# Optimizing a Trainium2 kernel written in Bass

```python
import numpy as np
import jax
import jax.numpy as jnp

def _softmax(x, axis=-1):
    return jax.nn.softmax(x, axis=axis)

def _gelu(x):
    return jax.nn.gelu(x, approximate=True)

def _silu(x):
    return jax.nn.silu(x)

def _sigmoid(x):
    return jax.nn.sigmoid(x)

def _layernorm(x, axis=-1, eps=1e-05):
    m = jnp.mean(x, axis=axis, keepdims=True)
    v = jnp.var(x, axis=axis, keepdims=True)
    return (x - m) / jnp.sqrt(v + eps)

def _scatter_add(tgt, idx, src, axis=0):
    return tgt.at[idx].add(src)

def _segment_sum(src, seg, n):
    return jax.ops.segment_sum(src, seg, n)
kernel_name = 'mk_decoder_postln_d1_seqx_r8_91e4fd'

def setup_inputs(seed: int=0):
    np.random.seed(seed)
    _w = jnp.asarray

    def _rec_inputs():
        import jax
        import jax.numpy as jnp
        _rk = jax.random.key(seed)
        x = 7.22e-05 + 1 * jax.random.normal(jax.random.fold_in(_rk, 1), (64, 64, 256), jnp.float32)
        _lenS = 64 - jax.random.randint(jax.random.fold_in(_rk, 7), (64,), 0, max(1, 64 // 4) + 1, jnp.int32)
        _lenS2 = 64 - jax.random.randint(jax.random.fold_in(_rk, 8), (64,), 0, max(1, 64 // 4) + 1, jnp.int32)
        _ctx_2048P = jax.random.normal(jax.random.fold_in(_rk, 11), (64, 16, 256), jnp.float32)
        _ctx_2048c = jax.random.dirichlet(jax.random.fold_in(_rk, 511), 0.3 * jnp.ones((16,), jnp.float32), (64, 64))
        _ctx_2048t = jnp.einsum('bsk,bkd->bsd', _ctx_2048c, _ctx_2048P)
        _ctx_2048t = _ctx_2048t * jax.lax.rsqrt(jnp.mean(jnp.square(_ctx_2048t)) + 1e-12) * 0.953939
        ctx_2048 = 4.13588e-05 + 0.999923 * (_ctx_2048t + 0.3 * jax.random.normal(jax.random.fold_in(_rk, 611), (64, 64, 256), jnp.float32))
        return (x, ctx_2048)
    x, ctx_2048 = _rec_inputs()

    def _L0_attn_setup():
        import jax, jax.numpy as jnp
        import numpy as np
        SCALE_BASE = 64
        EPS = 1e-05

        def _xpos_terms(seq_len, d):
            half = d // 2
            xscale = (jnp.arange(0, d, 2, dtype=jnp.float32) + 0.4 * d) / (1.4 * d)
            pos = jnp.arange(seq_len, dtype=jnp.float32)
            scale = xscale[None, :] ** (pos[:, None] / SCALE_BASE)
            inv_freq = 1.0 / 10000.0 ** (jnp.arange(half, dtype=jnp.float32) / half)
            sinu = pos[:, None] * inv_freq[None, :]
            return (jnp.sin(sinu), jnp.cos(sinu), scale)

        def _dup(t):
            return jnp.repeat(t, 2, axis=-1)

        def _rot(x):
            x1 = x[..., ::2]
            x2 = x[..., 1::2]
            return jnp.stack((-x2, x1), axis=-1).reshape(x.shape)

        def _apply_xpos(x, sin, cos, scale):
            c = _dup(cos * scale)
            s = _dup(sin * scale)
            return x * c + _rot(x) * s
        key = jax.random.key(seed)
        ks = jax.random.split(key, 6)
        B, S, H, nheads = (2, 128, 256, 16)
        d = H // nheads
        X = jax.random.normal(ks[0], (B, S, H), dtype=jnp.float32)
        W_Q = jax.random.normal(ks[1], (nheads, H, d), dtype=jnp.float32) / H
        W_K = jax.random.normal(ks[2], (nheads, H, d), dtype=jnp.float32) / H
        W_V = jax.random.normal(ks[3], (nheads, H, d), dtype=jnp.float32) / H
        W_G = jax.random.normal(ks[4], (H, H), dtype=jnp.float32) / H
        W_O = jax.random.normal(ks[5], (H, H), dtype=jnp.float32) / H
        gn_weight = jnp.ones((H,), dtype=jnp.float32)
        gn_bias = jnp.zeros((H,), dtype=jnp.float32)
        return {'X': X, 'W_Q': W_Q, 'W_K': W_K, 'W_V': W_V, 'W_G': W_G, 'W_O': W_O, 'gn_weight': gn_weight, 'gn_bias': gn_bias}
    _L0_attn_all = _L0_attn_setup()
    _L0_attn_in = {k: v for k, v in _L0_attn_all.items() if k in ('W_Q', 'W_K', 'W_V', 'W_G', 'W_O', 'gn_weight', 'gn_bias')}
    del _L0_attn_all

    def _L0_xattn_setup():
        import jax, jax.numpy as jnp
        import numpy as np
        import math
        EMBED = 256
        HEADS = 32
        GROUPS = 8
        GROUP_HEADS = HEADS // GROUPS
        HEAD_DIM = EMBED // HEADS
        B, S = (4, 128)
        key = jax.random.key(seed)
        ks = jax.random.split(key, 8)
        sc = 0.02
        return {'q': jax.random.normal(ks[0], (B, S, EMBED), jnp.float32), 'k': jax.random.normal(ks[1], (B, S, EMBED), jnp.float32), 'v': jax.random.normal(ks[2], (B, S, EMBED), jnp.float32), 'Wq': jax.random.normal(ks[3], (EMBED, EMBED), jnp.float32) * sc, 'Wk': jax.random.normal(ks[4], (GROUPS * HEAD_DIM, EMBED), jnp.float32) * sc, 'Wv': jax.random.normal(ks[5], (GROUPS * HEAD_DIM, EMBED), jnp.float32) * sc, 'Wfc': jax.random.normal(ks[6], (EMBED, EMBED), jnp.float32) * sc, 'bfc': jnp.zeros((EMBED,), jnp.float32)}
    _L0_xattn_all = _L0_xattn_setup()
    _L0_xattn_in = {k: v for k, v in _L0_xattn_all.items() if k in ('Wq', 'Wk', 'Wv', 'Wfc', 'bfc')}
    del _L0_xattn_all

    def _L0_ffn_setup():
        import jax, jax.numpy as jnp
        import numpy as np
        D_MODEL = 256
        D_FF = 1024

        def absmean_quant(w):
            scale = jnp.mean(jnp.abs(w))
            mask = (jnp.abs(w) >= scale * 0.7).astype(w.dtype)
            return jnp.sign(w) * mask
        key = jax.random.key(seed)
        k_x, k_w1, k_w2 = jax.random.split(key, 3)
        x = jax.random.normal(k_x, (4, 512, D_MODEL), dtype=jnp.float32)
        w1 = jax.random.normal(k_w1, (D_FF, D_MODEL), dtype=jnp.float32)
        b1 = jnp.zeros((D_FF,), dtype=jnp.float32)
        w2 = jax.random.normal(k_w2, (D_MODEL, D_FF), dtype=jnp.float32)
        b2 = jnp.zeros((D_MODEL,), dtype=jnp.float32)
        return {'x': x, 'w1': w1, 'b1': b1, 'w2': w2, 'b2': b2}
    _L0_ffn_all = _L0_ffn_setup()
    _L0_ffn_in = {k: v for k, v in _L0_ffn_all.items() if k in ('w1', 'b1', 'w2', 'b2')}
    del _L0_ffn_all
    return {'x': x, 'ctx_2048': ctx_2048, 'L0_attn_W_Q': _L0_attn_in['W_Q'], 'L0_attn_W_K': _L0_attn_in['W_K'], 'L0_attn_W_V': _L0_attn_in['W_V'], 'L0_attn_W_G': _L0_attn_in['W_G'], 'L0_attn_W_O': _L0_attn_in['W_O'], 'L0_attn_gn_weight': _L0_attn_in['gn_weight'], 'L0_attn_gn_bias': _L0_attn_in['gn_bias'], 'L0_xattn_Wq': _L0_xattn_in['Wq'], 'L0_xattn_Wk': _L0_xattn_in['Wk'], 'L0_xattn_Wv': _L0_xattn_in['Wv'], 'L0_xattn_Wfc': _L0_xattn_in['Wfc'], 'L0_xattn_bfc': _L0_xattn_in['bfc'], 'L0_ffn_w1': _L0_ffn_in['w1'], 'L0_ffn_b1': _L0_ffn_in['b1'], 'L0_ffn_w2': _L0_ffn_in['w2'], 'L0_ffn_b2': _L0_ffn_in['b2']}

def reference(x, ctx_2048, L0_attn_W_Q, L0_attn_W_K, L0_attn_W_V, L0_attn_W_G, L0_attn_W_O, L0_attn_gn_weight, L0_attn_gn_bias, L0_xattn_Wq, L0_xattn_Wk, L0_xattn_Wv, L0_xattn_Wfc, L0_xattn_bfc, L0_ffn_w1, L0_ffn_b1, L0_ffn_w2, L0_ffn_b2):
    import jax
    import jax.numpy as jnp

    def _L0_attn_ref(X, W_Q, W_K, W_V, W_G, W_O, gn_weight, gn_bias):
        import jax, jax.numpy as jnp
        import numpy as np
        SCALE_BASE = 64
        EPS = 1e-05

        def _xpos_terms(seq_len, d):
            half = d // 2
            xscale = (jnp.arange(0, d, 2, dtype=jnp.float32) + 0.4 * d) / (1.4 * d)
            pos = jnp.arange(seq_len, dtype=jnp.float32)
            scale = xscale[None, :] ** (pos[:, None] / SCALE_BASE)
            inv_freq = 1.0 / 10000.0 ** (jnp.arange(half, dtype=jnp.float32) / half)
            sinu = pos[:, None] * inv_freq[None, :]
            return (jnp.sin(sinu), jnp.cos(sinu), scale)

        def _dup(t):
            return jnp.repeat(t, 2, axis=-1)

        def _rot(x):
            x1 = x[..., ::2]
            x2 = x[..., 1::2]
            return jnp.stack((-x2, x1), axis=-1).reshape(x.shape)

        def _apply_xpos(x, sin, cos, scale):
            c = _dup(cos * scale)
            s = _dup(sin * scale)
            return x * c + _rot(x) * s
        B, S, H = X.shape
        nheads, _, d = W_Q.shape
        gammas = 1.0 - jnp.exp(jnp.linspace(np.log(1.0 / 32), np.log(1.0 / 64), nheads)).astype(jnp.float32)
        sin, cos, scale = _xpos_terms(S, d)
        Q = jnp.einsum('bsh,nhd->bnsd', X, W_Q)
        K = jnp.einsum('bsh,nhd->bnsd', X, W_K)
        V = jnp.einsum('bsh,nhd->bnsd', X, W_V)
        Q = _apply_xpos(Q, sin, cos, scale)
        K = _apply_xpos(K, sin, cos, 1.0 / scale)
        n = jnp.arange(S)[:, None]
        m = jnp.arange(S)[None, :]
        D = jnp.where(n >= m, gammas[:, None, None] ** (n - m).astype(jnp.float32), 0.0)
        ret = jnp.einsum('bnsd,bntd->bnst', Q, K) * D[None]
        Y = jnp.einsum('bnst,bntv->bnsv', ret, V)
        Y = jnp.transpose(Y, (0, 2, 1, 3)).reshape(B, S, nheads * d)
        Yg = Y.reshape(B, S, nheads, d)
        mu = Yg.mean(-1, keepdims=True)
        var = Yg.var(-1, keepdims=True)
        Yn = ((Yg - mu) / jnp.sqrt(var + EPS)).reshape(B, S, nheads * d)
        Yn = Yn * gn_weight + gn_bias
        G = X @ W_G
        gate = G * jax.nn.sigmoid(G)
        return gate * Yn @ W_O

    def _L0_xattn_ref(q, k, v, Wq, Wk, Wv, Wfc, bfc):
        import jax, jax.numpy as jnp
        import numpy as np
        import math
        EMBED = 256
        HEADS = 32
        GROUPS = 8
        GROUP_HEADS = HEADS // GROUPS
        HEAD_DIM = EMBED // HEADS
        B, S = (4, 128)
        N, S_, _ = q.shape
        qh = (q @ Wq.T).reshape(N, S_, HEADS, HEAD_DIM).transpose(0, 2, 1, 3)
        kh = (k @ Wk.T).reshape(N, S_, GROUPS, HEAD_DIM).transpose(0, 2, 1, 3)
        vh = (v @ Wv.T).reshape(N, S_, GROUPS, HEAD_DIM).transpose(0, 2, 1, 3)
        kh = jnp.repeat(kh, GROUP_HEADS, axis=1)
        vh = jnp.repeat(vh, GROUP_HEADS, axis=1)
        score = jnp.einsum('bhqd,bhkd->bhqk', qh, kh) / math.sqrt(HEAD_DIM)
        attn = jax.nn.softmax(score, axis=-1)
        out = jnp.einsum('bhqk,bhkd->bhqd', attn, vh)
        out = out.transpose(0, 2, 1, 3).reshape(N, S_, EMBED)
        return out @ Wfc.T + bfc

    def _L0_ffn_ref(x, w1, b1, w2, b2):
        import jax, jax.numpy as jnp
        import numpy as np
        D_MODEL = 256
        D_FF = 1024

        def absmean_quant(w):
            scale = jnp.mean(jnp.abs(w))
            mask = (jnp.abs(w) >= scale * 0.7).astype(w.dtype)
            return jnp.sign(w) * mask
        w1_q = absmean_quant(w1)
        w2_q = absmean_quant(w2)
        h = jnp.einsum('bsd,fd->bsf', x, w1_q) + b1
        h = jax.nn.gelu(h, approximate=False)
        out = jnp.einsum('bsf,df->bsd', h, w2_q) + b2
        return out
    x = _layernorm(x + _L0_attn_ref(x, L0_attn_W_Q, L0_attn_W_K, L0_attn_W_V, L0_attn_W_G, L0_attn_W_O, L0_attn_gn_weight, L0_attn_gn_bias), axis=-1)
    x = _layernorm(x + _L0_xattn_ref(x, ctx_2048, ctx_2048, L0_xattn_Wq, L0_xattn_Wk, L0_xattn_Wv, L0_xattn_Wfc, L0_xattn_bfc), axis=-1)
    x = _layernorm(x + _L0_ffn_ref(x, L0_ffn_w1, L0_ffn_b1, L0_ffn_w2, L0_ffn_b2), axis=-1)
    return x

_drawn_inputs = setup_inputs


def setup_inputs(seed=0):
    import zlib

    import numpy as np

    out = dict(_drawn_inputs(seed))
    spreads = {'L0_attn_gn_weight': (1.0, 0.6),
     'L0_attn_gn_bias': (0.0, 0.8),
     'L0_xattn_bfc': (0.0, 0.1),
     'L0_ffn_b1': (0.0, 0.8),
     'L0_ffn_b2': (0.0, 0.8)}
    factors = {'L0_attn_W_Q': 8.0,
     'L0_attn_W_K': 8.0,
     'L0_attn_W_V': 8.0,
     'L0_attn_W_G': 8.0,
     'L0_attn_W_O': 8.0,
     'L0_xattn_Wq': 8.0,
     'L0_xattn_Wk': 8.0}
    for name, (base, spread) in spreads.items():
        noise = np.random.default_rng([zlib.crc32(name.encode()), seed]).standard_normal(out[name].shape)
        drawn = base * np.exp(spread * noise) if base else spread * noise
        out[name] = jnp.asarray(drawn.astype(out[name].dtype))
    for name, factor in factors.items():
        out[name] = (out[name] * factor).astype(out[name].dtype)
    return out
```

```python
from contextlib import ExitStack

import numpy as np

import concourse.bass as bass
from concourse import mybir
from concourse.alu_op_type import AluOpType as ALU

F32 = mybir.dt.float32
F32R = mybir.dt.float32r
ACT = mybir.ActivationFunctionType
AX = mybir.AxisListType

SEQS, SEQ, D = 64, 64, 256
TOKENS = SEQS * SEQ
P = 128
KC = D // P
TB = 256
TP = TB // P
BS = TB // SEQ
NB = TOKENS // TB
HEADS, HD = 16, 16
XHEADS, XG, XD = 32, 8, 8
XJ = XHEADS // XG
F = 1024
FC = F // P
EPS = 1e-5
ATTN_EPS = 1e-5
LAG_GATE, LAG_CROSS, LAG_FFN = 1, 2, 3


def shape_constants():
    f = np.float32
    half = HD // 2
    xscale = (np.arange(0, HD, 2, dtype=f) + f(0.4 * HD)) / f(1.4 * HD)
    pos = np.arange(SEQ, dtype=f)
    scale = xscale[None, :] ** (pos[:, None] / f(64))
    inv = f(1.0) / f(10000.0) ** (np.arange(half, dtype=f) / f(half))
    angle = pos[:, None] * inv[None, :]
    p = np.arange(P)
    pair = (p % HD) // 2
    xpos = np.stack([(np.cos(angle) * scale)[:, pair].T, (np.sin(angle) * scale)[:, pair].T,
                     (np.cos(angle) * (f(1) / scale))[:, pair].T,
                     (np.sin(angle) * (f(1) / scale))[:, pair].T], 1).astype(f)
    gammas = f(1) - np.exp(np.linspace(np.log(1.0 / 32), np.log(1.0 / 64), HEADS)).astype(f)
    b, t = p // SEQ, p % SEQ
    decay = np.zeros((P, 4, KC, 2, P), f)
    lag = (t[None, :] - t[:, None])
    seen = (b[None, :] == b[:, None]) & (lag >= 0)
    for r in range(4):
        for c in range(KC):
            for par in range(2):
                g = gammas[8 * c + 2 * r + par]
                decay[:, r, c, par] = np.where(seen, g ** np.maximum(lag, 0).astype(f), 0)
    small = np.zeros((P, 14), f)
    for par in range(2):
        small[:, par] = (p // HD) % 2 == par
    for j in range(XJ):
        small[:, 2 + j] = (p % 32) // XD == j
    mats = np.zeros((P, 4, P), f)
    mats[:, 0] = np.eye(P)
    mats[:, 1] = (p[:, None] // HD == p[None, :] // HD) / HD
    for s in range(2):
        mats[:, 2 + s] = (b[:, None] == s) & (t[:, None] == t[None, :])
    ones = np.zeros((P, 2, 32), f)
    for jj in range(2):
        ones[:, jj] = np.arange(32)[None, :] // XD == 2 * jj + b[:, None]
    small[:, 6:14] = (p[:, None] // HD == np.arange(8)[None, :]) / HD
    spread = np.zeros((P, 4, P), f)
    for tc in range(4):
        for h in range(8):
            spread[8 * tc + h, tc] = p // HD == h
    return {"c_spread": spread.reshape(P, -1), "c_xpos": xpos, "c_decay": decay.reshape(P, -1), "c_small": small,
            "c_mats": mats.reshape(P, -1), "c_ones": ones.reshape(P, -1)}


def build(nc, x, ctx, wq, wk, wv, wg, wo, gnw, gnb, xwq, xwk, xwv, xwfc, xbfc, w1, b1, w2, b2,
          c_xpos, c_decay, c_small, c_mats, c_ones, c_spread, out):
    x_blocks = x.rearrange("(n t p) c -> n p t c", p=P, t=TP)
    ctx_blocks = ctx.rearrange("(n t p) c -> n p t c", p=P, t=TP)
    out_blocks = out.rearrange("(n t p) c -> n p t c", p=P, t=TP)

    stack = ExitStack()
    with stack:
        def sb(name, shape, dt=F32):
            return stack.enter_context(nc.sbuf_tensor(name, shape, dt))

        def ps(name, shape, dt=F32):
            return stack.enter_context(nc.psum_tensor(name, shape, dt))

        def sem(name):
            return stack.enter_context(nc.semaphore(name))

        NW = 8
        w_hi = sb("w_hi", [P, NW, KC, D], F32R)
        w_lo = sb("w_lo", [P, NW, KC, D], F32R)
        wxv_hi = sb("wxv_hi", [P, KC, XG * XD], F32R)
        wxv_lo = sb("wxv_lo", [P, KC, XG * XD], F32R)
        wo_sb = sb("wo_sb", [P, KC, D])
        wfc_sb = sb("wfc_sb", [P, KC, D])
        w1q = sb("w1q", [P, KC, F], F32R)
        w2q = sb("w2q", [P, FC, D], F32R)
        xpos = sb("xpos", [P, 4, SEQ])
        decay = sb("decay", [P, 2 * KC * 4 * P])
        small = sb("small", [P, 14])
        spread = sb("spread", [32, 4, P])
        mats = sb("mats", [P, 4, P])
        ones = sb("ones", [P, 2, 32])
        gn_w = sb("gn_w", [P, KC])
        gn_b = sb("gn_b", [P, KC])
        b1_sb = sb("b1_sb", [P, FC])
        bfc_sb = sb("bfc_sb", [P, D])
        b2_sb = sb("b2_sb", [P, D])
        all_mean = sb("all_mean", [P, P])
        abs_sum = sb("abs_sum", [P, 2])
        thr = sb("thr", [P, 2, 2])

        x_in = sb("x_in", [P, TP, D])
        ctx_in = sb("ctx_in", [P, TP, D])
        x_res = sb("x_res", [P, TP, D])
        xT_hi, xT_lo = sb("xT_hi", [P, KC, TB], F32R), sb("xT_lo", [P, KC, TB], F32R)
        cT_hi, cT_lo = sb("cT_hi", [P, KC, TB], F32R), sb("cT_lo", [P, KC, TB], F32R)
        x1T_hi, x1T_lo = sb("x1T_hi", [P, KC, TB], F32R), sb("x1T_lo", [P, KC, TB], F32R)
        x2T_hi, x2T_lo = sb("x2T_hi", [P, KC, TB], F32R), sb("x2T_lo", [P, KC, TB], F32R)
        q_cos = sb("q_cos", [P, KC, TB])
        k_all = sb("k_all", [P, KC, TB])
        rot_sin = sb("rot_sin", [P, KC, TB])
        q_par = sb("q_par", [P, 2, KC, TB])
        v_par = sb("v_par", [P, 2, TP, D])
        rT = sb("rT", [P, TP, 4, KC, 2, P])
        gate_th = sb("gate_th", [P, KC, TB])
        gate_sb = sb("gate_sb", [P, KC, TB])
        y_sb = sb("y_sb", [P, KC, TB])
        y_mid = sb("y_mid", [P, KC, TB])
        y_sq = sb("y_sq", [P, KC, TB])
        y_var = sb("y_var", [P, TP * KC * 8])
        y_rstd = sb("y_rstd", [P, TP * KC * 8])
        y_rstdT = sb("y_rstdT", [TP * KC * 8, P])
        y_norm = sb("y_norm", [P, KC, TB])
        carrier = sb("carrier", [P, 16])
        minus_half = sb("minus_half", [P, TP * KC * 8])
        zT = sb("zT", [P, KC, TB])
        bn6 = sb("bn6", [P, 3, TP, 6])
        bn2 = sb("bn2", [P, 3, TP, 2])
        rstd = sb("rstd", [P, 3, TP])
        x1 = sb("x1", [P, TP, D])
        x1_b = sb("x1_b", [P, TP, D])
        x2 = sb("x2", [P, TP, D])
        x2_b = sb("x2_b", [P, TP, D])
        y_out = sb("y_out", [P, TP, D])
        qx = sb("qx", [P, KC, TB])
        kx = sb("kx", [P, KC, BS, XJ, SEQ])
        vx = sb("vx", [P, TP, XG * XD])
        vx_bd = sb("vx_bd", [P, 2 * TP, XG, 2, 32])
        e_sb = sb("e_sb", [P, XHEADS, SEQ])
        e_max = sb("e_max", [P, XHEADS])
        pT = sb("pT", [P, 4, KC, 2, P])
        oT = sb("oT", [P, TP, KC, P])
        h_sb = sb("h_sb", [P, FC, TB])
        h_hi, h_lo = sb("h_hi", [P, FC, TB], F32R), sb("h_lo", [P, FC, TB], F32R)
        r_flat = rT[:, :, :, :, :, :].rearrange("p t r c q s -> p (t r c q s)")
        raw = r_flat[:, 0:5 * KC * D].rearrange("p (w k n) -> p w k n", w=5, k=KC)
        raw_kv = r_flat[:, 5 * KC * D:5 * KC * D + 2 * KC * XG * XD]\
            .rearrange("p (w k n) -> p w k n", w=2, k=KC)
        w1_raw = e_sb[:, :, :].rearrange("p a b -> p (a b)")
        w2_raw = h_sb[:, :, :].rearrange("p a b -> p (a b)")
        w_scr = pT[:, :, :, :, :].rearrange("p a b c d -> p (a b c d)")

        bank = [ps(f"bank{k}", [P, 2, 256]) for k in range(4)]
        big = ps("big", [P, 4, 2, 256])

        names = """w_in c_in bias_in h_hi w_split w_quant1 w_quant2 w_abs w_abs_all w_thr w_zero w_ge w_acc
            x_load c_load x_store
            xT cT x1T x2T mu q qr xq var k kr s0 v g rt rx o1 f0 f1 f2 f3 t0 kx_ps vx_ps s1 pv0 f_out t1
            r0 pv1 vd o2 r1 av
            xTh cTh x1Th x2Th sqd qx_sb v_sb th e0 e1 h0 h1 h2 h3 p0a p1a vx_sb vbd y_ev
            xTl cTl x1Tl x2Tl ymid qcos qsin yn rt_sb veps kcos ksin m0 m1 d0 d1 z gp a1 st1 ag1 x1d
            p0b p1b kx_sb rd0 rd1 o0d o1d a3 st3 ag3 y3d rm0 rm1 a2 st2 ag2 x2d
            gmove x1b x2b qadd qpar yeps ypow ep1 ep2 ep3 po1 po2 po3 yaff kadd hs0 hs1 hs2 hs3 xres""".split()
        S = {n: sem(n) for n in names}
        block = stack.enter_context(nc.Block())

        def done(eng, name, i, lag=0):
            n = i - lag
            if isinstance(n, int):
                n = min(n, NB - 1)
                if n < 0:
                    return
            eng.wait_ge(S[name], n + 1)

        def freed(eng, i, *users):
            for name, lag in users:
                n = i - lag
                if not isinstance(n, int) or 0 <= n < NB:
                    eng.wait_ge(S[name], n + 1)
                    return

        def iterations(eng, one):
            def act(i):
                return [0 <= i - lag < NB for lag in range(4)]
            for i in range(LAG_FFN + 1):
                one(i, act(i))
            with eng.Fori(LAG_FFN + 1, NB) as i:
                one(i, [True] * 4)
            for i in range(NB, NB + LAG_FFN):
                one(i, act(i))

        ident = mats[:, 0, :]
        head_mean = mats[:, 1, :]

        @block.sync
        def _(eng):
            for k, w in enumerate((wq, wk, wv, wg, xwq)):
                eng.dma_start(raw[:, k, :, :], w.rearrange("(k p) n -> p k n", p=P)).then_inc(S["w_in"], 16)
            for k, w in enumerate((xwk, xwv)):
                eng.dma_start(raw_kv[:, k, :, :], w.rearrange("(k p) n -> p k n", p=P)).then_inc(S["w_in"], 16)
            eng.dma_start(w1_raw.rearrange("p (k n) -> p k n", k=KC),
                          w1.rearrange("(k p) n -> p k n", p=P)).then_inc(S["w_in"], 16)
            eng.dma_start(w2_raw.rearrange("p (k n) -> p k n", k=FC),
                          w2.rearrange("(k p) n -> p k n", p=P)).then_inc(S["w_in"], 16)

            def one(i, on):
                ret, gate, cross, ffn = on
                if ret:
                    done(eng, "xT", i, 1)
                    done(eng, "xres", i, 1)
                    eng.dma_start(x_in[:, :, :], x_blocks[i, :, :, :]).then_inc(S["x_load"], 16)
                if gate:
                    n = i - LAG_GATE
                    done(eng, "cT", n, 1)
                    eng.dma_start(ctx_in[:, :, :], ctx_blocks[n, :, :, :]).then_inc(S["c_load"], 16)
                if ffn:
                    n = i - LAG_FFN
                    done(eng, "y3d", n)
                    eng.dma_start(out_blocks[n, :, :, :], y_out[:, :, :]).then_inc(S["x_store"], 16)
            iterations(eng, one)
            eng.wait_ge(S["x_store"], 16 * NB)

        @block.tensor
        def _(eng):
            def flat(k):
                return bank[k][:, :, :].rearrange("p a b -> p (a b)")

            def transposes(src, k, step):
                for c in range(KC):
                    for t in range(TP):
                        mm = eng.transpose(bank[k][:, c, t * P:(t + 1) * P],
                                           src[:, t, c * P:(c + 1) * P], ident)
                mm.then_inc(S[step], 1)

            def split_product(o, parts, last, step=None):
                for n, (w, a) in enumerate(parts):
                    mm = eng.matmul(o, w, a, start=(n == 0), stop=(n == len(parts) - 1))
                if last:
                    mm.then_inc(S[step], 1)

            def project(w, hi, lo, k, step):
                for oc in range(KC):
                    cols = slice(oc * P, (oc + 1) * P)
                    parts = [(a[:, w, kc, cols], b[:, kc, :])
                             for a, b in ((w_lo, hi), (w_hi, lo), (w_hi, hi)) for kc in range(KC)]
                    split_product(bank[k][:, oc, :], parts, oc == KC - 1, step)

            def out_rows(act, w, k, step):
                for t in range(TP):
                    for kc in range(KC):
                        mm = eng.matmul(bank[k][:, t, :], act(t, kc), w[:, kc, :],
                                        start=(kc == 0), stop=(kc == KC - 1))
                mm.then_inc(S[step], 1)

            def ret_scores(t, step):
                for c in range(KC):
                    for par in range(2):
                        for r in range(4):
                            rows = slice(32 * r, 32 * r + 32)
                            col = (c * 2 + par) * P
                            mm = eng.matmul(big[:, r, :, :].rearrange("p a b -> p (a b)")[:, col:col + P],
                                            k_all[rows, c, t * P:(t + 1) * P],
                                            q_par[rows, par, c, t * P:(t + 1) * P], start=True, stop=True)
                mm.then_inc(S[step], 1)

            def cross_scores(t, step):
                for c in range(KC):
                    for r in range(4):
                        rows = slice(32 * r, 32 * r + 32)
                        for b in range(2):
                            tok = (2 * t + b) * SEQ
                            mm = eng.matmul(big[b * SEQ:(b + 1) * SEQ, r, c, :], qx[rows, c, tok:tok + SEQ],
                                            kx[rows, c, 2 * t + b, :, :].rearrange("p j s -> p (j s)"),
                                            start=True, stop=True)
                mm.then_inc(S[step], 1)

            def rstd_spread(g):
                done(eng, "rt_sb", g)
                for t in range(TP):
                    for c in range(KC):
                        mm = eng.matmul(bank[2][:, c, t * P:(t + 1) * P], spread[:, t * KC + c, :],
                                        y_rstdT[:, :], start=True, stop=True)
                mm.then_inc(S["rx"], 1)

            def prob_transposes(step):
                for r in range(4):
                    for q in range(4):
                        mm = eng.transpose(big[:, r, :, :].rearrange("p a b -> p (a b)")[:, q * P:(q + 1) * P],
                                           e_sb[:, :, :].rearrange("p h s -> p (h s)")
                                           [:, (4 * r + q) * P:(4 * r + q + 1) * P], ident)
                mm.then_inc(S[step], 1)

            def prob_values(t, k, step):
                for c in range(KC):
                    for b in range(2):
                        for jj in range(2):
                            for r in range(4):
                                eng.matmul(bank[k][32 * r:32 * r + 32, 0, c * P + b * SEQ:c * P + (b + 1) * SEQ],
                                           vx_bd[:, b * TP + t, 4 * c + r, jj, :],
                                           pT[:, r, c, jj, b * SEQ:(b + 1) * SEQ],
                                           start=(jj == 0), stop=(jj == 1), tile_position=(0, 32 * r))
                    for jj in range(2):
                        for r in range(4):
                            mm = eng.matmul(bank[k][32 * r:32 * r + 32, 1, c * P:(c + 1) * P],
                                            ones[:, jj, :], pT[:, r, c, jj, :],
                                            start=(jj == 0), stop=(jj == 1), tile_position=(0, 32 * r))
                mm.then_inc(S[step], 1)

            eng.wait_ge(S["w_abs"], 2)
            eng.wait_ge(S["w_zero"], 3)
            eng.matmul(bank[0][:, 0, 0:2], all_mean[:, :], abs_sum[:, :], start=True, stop=True)\
               .then_inc(S["w_abs_all"], 1)
            eng.wait_ge(S["c_in"], 16 * 11)
            eng.wait_ge(S["w_split"], 1)
            eng.wait_ge(S["w_quant1"], 1)
            eng.wait_ge(S["w_quant2"], 1)

            def one(i, on):
                ret, gate, cross, ffn = on
                g, b, f = i - LAG_GATE, i - LAG_CROSS, i - LAG_FFN
                if ret:
                    eng.wait_ge(S["x_load"], 16 * i + 16)
                    freed(eng, i, ("o1d", 3), ("h2", 4), ("v_sb", 1))
                    transposes(x_in, 0, "xT")
                if gate:
                    eng.wait_ge(S["c_load"], 16 * g + 16)
                    freed(eng, i, ("y_ev", 1), ("a3", 4))
                    transposes(ctx_in, 1, "cT")
                if cross:
                    done(eng, "x1d", b)
                    freed(eng, i, ("a2", 3), ("a1", 2))
                    transposes(x1, 2, "x1T")
                if ffn:
                    done(eng, "x2d", f)
                    freed(eng, i, ("vbd", 2), ("h1", 4))
                    transposes(x2, 3, "x2T")
                if gate:
                    done(eng, "y_ev", g)
                    freed(eng, i, ("xTl", 0), ("o1d", 3), ("v_sb", 1))
                    eng.matmul(flat(0), head_mean, y_sb[:, :, :].rearrange("p a b -> p (a b)"),
                               start=True, stop=True).then_inc(S["mu"], 1)
                if ret:
                    done(eng, "xTl", i)
                    freed(eng, i, ("cTl", 1), ("y_ev", 1))
                    project(0, xT_hi, xT_lo, 1, "q")
                    freed(eng, i, ("x1Tl", 2), ("a1", 2))
                    project(1, xT_hi, xT_lo, 2, "qr")
                if cross:
                    done(eng, "x1Tl", b)
                    freed(eng, i, ("x2Tl", 3), ("vbd", 2))
                    project(6, x1T_hi, x1T_lo, 3, "xq")
                if gate:
                    done(eng, "sqd", g)
                    done(eng, "ymid", g)
                    for t in range(TP):
                        for c in range(KC):
                            mm = eng.matmul(bank[0][:, 0, (t * KC + c) * 8:(t * KC + c + 1) * 8],
                                            y_sq[:, c, t * P:(t + 1) * P], small[:, 6:14],
                                            start=True, stop=True)
                    mm.then_inc(S["var"], 1)
                if ret:
                    done(eng, "qcos", i)
                    project(2, xT_hi, xT_lo, 1, "k")
                    done(eng, "qsin", i)
                    project(3, xT_hi, xT_lo, 2, "kr")
                if cross:
                    done(eng, "qx_sb", b)
                    done(eng, "kx_sb", b)
                    freed(eng, i, ("rm1", 1), ("p1b", 3))
                    cross_scores(0, "s0")
                if ret:
                    freed(eng, i, ("veps", 1), ("xTl", 0))
                    for t in range(TP):
                        parts = [(a[:, kc, t * P:(t + 1) * P], w[:, 5, kc, :])
                                 for a, w in ((xT_lo, w_hi), (xT_hi, w_lo), (xT_hi, w_hi))
                                 for kc in range(KC)]
                        split_product(bank[0][:, t, :], parts, t == TP - 1, "v")
                    done(eng, "kcos", i)
                    project(4, xT_hi, xT_lo, 1, "g")
                if gate:
                    done(eng, "ypow", g)
                    freed(eng, i, ("ksin", 0), ("x1Tl", 2), ("a1", 2))
                    eng.transpose(bank[2][0:32, 0, 0:P], y_rstd[:, :], ident).then_inc(S["rt"], 1)
                if ffn:
                    done(eng, "x2Tl", f)
                    for u, (k, before) in enumerate((
                            (3, (("qx_sb", 2), ("x2Tl", 3))),
                            (3, (("h0", 3),)),
                            (0, (("v_sb", 0), ("veps", 1), ("o1d", 3))),
                            (1, (("gp", 0), ("cTl", 1), ("a3", 4))))):
                        freed(eng, i, *before)
                        if u == 2 and gate:
                            rstd_spread(g)
                        for oc in range(2):
                            fc = 2 * u + oc
                            parts = [(w1q[:, kc, fc * P:(fc + 1) * P], a[:, kc, :])
                                     for a in (x2T_lo, x2T_hi) for kc in range(KC)]
                            split_product(bank[k][:, oc, :], parts, oc == 1, f"f{u}")
                if gate and not ffn:
                    rstd_spread(g)
                if cross:
                    done(eng, "e0", b)
                    done(eng, "d0", b)
                    prob_transposes("t0")
                if gate:
                    done(eng, "cTl", g)
                    done(eng, "yn", g)
                    project(7, cT_hi, cT_lo, 2, "kx_ps")
                    freed(eng, i, ("h1", 3), ("qx_sb", 2), ("vbd", 2))
                    for t in range(TP):
                        parts = [(a[:, kc, t * P:(t + 1) * P], w[:, kc, :])
                                 for a, w in ((cT_lo, wxv_hi), (cT_hi, wxv_lo), (cT_hi, wxv_hi))
                                 for kc in range(KC)]
                        split_product(bank[3][:, 0, t * 64:(t + 1) * 64], parts, t == TP - 1, "vx_ps")
                if cross:
                    done(eng, "p0a", b)
                    done(eng, "p0b", b)
                    cross_scores(1, "s1")
                    freed(eng, i, ("h2", 3), ("v_sb", 0), ("veps", 1), ("o1d", 3))
                    done(eng, "vbd", b)
                    prob_values(0, 0, "pv0")
                if ffn:
                    freed(eng, i, ("h3", 3))
                    for t in range(TP):
                        n = 0
                        for fc in range(FC):
                            if t == 0 and fc % 2 == 0:
                                done(eng, f"hs{fc // 2}", f)
                            for a in (h_lo, h_hi):
                                mm = eng.matmul(bank[1][:, t, :], a[:, fc, t * P:(t + 1) * P], w2q[:, fc, :],
                                                start=(n == 0), stop=(n == 2 * FC - 1))
                                n += 1
                    mm.then_inc(S["f_out"], 1)
                if gate:
                    done(eng, "z", g)
                    done(eng, "kx_sb", g)
                    out_rows(lambda t, kc: zT[:, kc, t * P:(t + 1) * P], wo_sb, 2, "o1")
                if cross:
                    done(eng, "e1", b)
                    done(eng, "d1", b)
                    prob_transposes("t1")
                if ret:
                    done(eng, "qpar", i)
                    done(eng, "kadd", i)
                    freed(eng, i, ("p1b", 2), ("rm1", 1))
                    if not (isinstance(i, int) and not cross):
                        done(eng, "p1a", b)
                    ret_scores(0, "r0")
                if cross:
                    done(eng, "p1a", b)
                    done(eng, "p1b", b)
                    done(eng, "o0d", b)
                    prob_values(1, 0, "pv1")
                if gate:
                    done(eng, "vx_sb", g)
                    for s in range(2):
                        mm = eng.matmul(bank[3][:, 1, s * P:(s + 1) * P], mats[:, 2 + s, :],
                                        vx[:, :, :].rearrange("p t c -> p (t c)"), start=True, stop=True)
                    mm.then_inc(S["vd"], 1)
                if cross:
                    done(eng, "o1d", b)
                    freed(eng, i, ("a1", 1), ("x1Tl", 2))
                    out_rows(lambda t, kc: oT[:, t, kc, :], wfc_sb, 2, "o2")
                if ret:
                    done(eng, "rm0", i)
                    ret_scores(1, "r1")
                    freed(eng, i, ("a3", 3), ("gp", 0))
                    for t in range(TP):
                        if t == 1:
                            done(eng, "rm1", i)
                        for c in range(KC):
                            for par in range(2):
                                for r in range(4):
                                    mm = eng.matmul(bank[1][32 * r:32 * r + 32, c, t * P:(t + 1) * P],
                                                    v_par[:, par, t, c * P + 32 * r:c * P + 32 * r + 32],
                                                    rT[:, t, r, c, par, :],
                                                    start=(par == 0), stop=(par == 1),
                                                    tile_position=(0, 32 * r))
                    mm.then_inc(S["av"], 1)
            iterations(eng, one)

        @block.scalar
        def _(eng):
            def copy(o, a):
                return eng.activation(o, a, ACT.Copy)

            eng.dma_start(mats[:, :, :].rearrange("p a b -> p (a b)"), c_mats).then_inc(S["c_in"], 16)
            eng.dma_start(spread[:, :, :].rearrange("p a b -> p (a b)"), c_spread[0:32, :]).then_inc(S["c_in"], 16)
            eng.dma_start(small[:, :], c_small).then_inc(S["c_in"], 16)
            eng.dma_start(xpos[:, :, :].rearrange("p a b -> p (a b)"),
                          c_xpos.rearrange("p a b -> p (a b)")).then_inc(S["c_in"], 16)
            eng.dma_start(decay[:, :], c_decay).then_inc(S["c_in"], 16)
            eng.dma_start(ones[:, :, :].rearrange("p a b -> p (a b)"), c_ones).then_inc(S["c_in"], 16)
            eng.dma_start(wo_sb[:, :, :], wo.rearrange("(k p) n -> p k n", p=P)).then_inc(S["c_in"], 16)
            eng.dma_start(wfc_sb[:, :, :], xwfc.rearrange("(k p) n -> p k n", p=P)).then_inc(S["c_in"], 16)
            eng.dma_start(b1_sb[:, :], b1).then_inc(S["c_in"], 16)
            eng.dma_start(gn_w[:, :], gnw).then_inc(S["c_in"], 16)
            eng.dma_start(gn_b[:, :], gnb).then_inc(S["c_in"], 16)

            eng.wait_ge(S["w_zero"], 3)
            eng.wait_ge(S["c_in"], 16 * 11)

            def one(i, on):
                ret, gate, cross, ffn = on
                g, b, f = i - LAG_GATE, i - LAG_CROSS, i - LAG_FFN
                if ret:
                    done(eng, "xT", i)
                    done(eng, "g", i, 1)
                    copy(xT_hi[:, :, :], bank[0][:, :, :]).then_inc(S["xTh"], 1)
                if gate:
                    done(eng, "cT", g)
                    done(eng, "vx_ps", g, 1)
                    copy(cT_hi[:, :, :], bank[1][:, :, :]).then_inc(S["cTh"], 1)
                if cross:
                    done(eng, "x1T", b)
                    done(eng, "xq", b, 1)
                    copy(x1T_hi[:, :, :], bank[2][:, :, :]).then_inc(S["x1Th"], 1)
                if ffn:
                    done(eng, "x2T", f)
                    done(eng, "f3", f, 1)
                    copy(x2T_hi[:, :, :], bank[3][:, :, :]).then_inc(S["x2Th"], 1)
                if gate:
                    done(eng, "ymid", g)
                    done(eng, "var", g, 1)
                    eng.activation(y_sq[:, :, :], y_mid[:, :, :], ACT.Square).then_inc(S["sqd"], 1)
                if cross:
                    done(eng, "xq", b)
                    done(eng, "s1", b, 1)
                    copy(qx[:, :, :], bank[3][:, :, :]).then_inc(S["qx_sb"], 1)
                if ret:
                    done(eng, "v", i)
                    done(eng, "av", i, 1)
                    for par in range(2):
                        cols = [t_[:, :, :].rearrange("p t (h c) -> p (t h) c", c=2 * HD)[:, :, par * HD:par * HD + HD]
                                for t_ in (v_par[:, par, :, :], bank[0][:, :, :])]
                        mm = copy(cols[0], cols[1])
                    mm.then_inc(S["v_sb"], 1)
                    done(eng, "g", i)
                    done(eng, "gmove", i, 1)
                    eng.activation(gate_th[:, :, :], bank[1][:, :, :], ACT.Tanh, scale=0.5)\
                       .then_inc(S["th"], 1)
                if cross:
                    done(eng, "d0", b)
                    eng.activation(e_sb[:, :, :], e_sb[:, :, :], ACT.Exp, scale=float(XD) ** -0.5)\
                       .then_inc(S["e0"], 1)
                if ffn:
                    for u, k in enumerate((3, 3, 0, 1)):
                        done(eng, f"f{u}", f)
                        done(eng, f"hs{u}", f, 1)
                        for oc in range(2):
                            fc = 2 * u + oc
                            mm = eng.activation(h_sb[:, fc, :], bank[k][:, oc, :], ACT.Gelu,
                                                bias=b1_sb[:, fc:fc + 1])
                        mm.then_inc(S[f"h{u}"], 1)
                if cross:
                    done(eng, "t0", b)
                    done(eng, "pv1", b, 1)
                    copy(pT[:, 0:2, :, :, :].rearrange("p r a b c -> p (r a b c)"),
                         big[:, 0:2, :, :].rearrange("p r a b -> p (r a b)")).then_inc(S["p0a"], 1)
                if gate:
                    done(eng, "vx_ps", g)
                    done(eng, "vd", g, 1)
                    copy(vx[:, :, :].rearrange("p t c -> p (t c)"), bank[3][:, 0, 0:P]).then_inc(S["vx_sb"], 1)
                if cross:
                    done(eng, "d1", b)
                    eng.activation(e_sb[:, :, :], e_sb[:, :, :], ACT.Exp, scale=float(XD) ** -0.5)\
                       .then_inc(S["e1"], 1)
                    done(eng, "t1", b)
                    done(eng, "pv0", b)
                    copy(pT[:, 0:2, :, :, :].rearrange("p r a b c -> p (r a b c)"),
                         big[:, 0:2, :, :].rearrange("p r a b -> p (r a b)")).then_inc(S["p1a"], 1)
                if gate:
                    done(eng, "vd", g)
                    done(eng, "pv1", g, 1)
                    for h in range(2):
                        rows = slice(h * SEQ, (h + 1) * SEQ)
                        src = bank[3][rows, 1, :].rearrange("p (a d) -> p a d", d=XD)
                        for jj in range(2):
                            mm = copy(vx_bd[rows, :, :, jj, (2 * jj + h) * XD:(2 * jj + h + 1) * XD]
                                      .rearrange("p a g d -> p (a g) d"), src)
                    mm.then_inc(S["vbd"], 1)
                if ret:
                    done(eng, "av", i)
                    done(eng, "ymid", i, 1)
                    copy(y_sb[:, :, :], bank[1][:, :, :]).then_inc(S["y_ev"], 1)
            iterations(eng, one)

        @block.vector
        def _(eng):
            def bcast(ap, axis, n):
                a = ap.unsqueeze(axis)
                shape = list(a.shape)
                shape[axis] = n
                return a.to_broadcast(shape)

            eng.wait_ge(S["w_in"], 16 * 9)
            for k, r_ in enumerate((w1_raw, w2_raw)):
                eng.tensor_reduce(abs_sum[:, k:k + 1], r_, AX.X, ALU.add, apply_absolute_value=True)\
                   .then_inc(S["w_abs"], 1)
            order = (0, None, 1, None, 3, 2, 4)
            for k, src in enumerate(order):
                if src is not None:
                    eng.tensor_copy(w_hi[:, k, :, :], raw[:, src, :, :]).then_inc(S["w_acc"], 1)
            for k, src in ((1, 0), (3, 1)):
                pairs = raw[:, src, :, :].rearrange("p k (a b) -> p (k a) b", b=2)
                dst = w_hi[:, k, :, :].rearrange("p k (a b) -> p (k a) b", b=2)
                eng.tensor_scalar(dst[:, :, 0], pairs[:, :, 1], -1.0, None, ALU.mult).then_inc(S["w_acc"], 1)
                eng.tensor_copy(dst[:, :, 1], pairs[:, :, 0]).then_inc(S["w_acc"], 1)
            kx_rep = bcast(raw_kv[:, 0, :, :].rearrange("p k (g d) -> p (k g) d", d=XD), 2, XJ)
            kx_hi = w_hi[:, 7, :, :].rearrange("p k (g j d) -> p (k g) j d", j=XJ, d=XD)
            kx_lo = w_lo[:, 7, :, :].rearrange("p k (g j d) -> p (k g) j d", j=XJ, d=XD)
            eng.tensor_copy(kx_hi, kx_rep).then_inc(S["w_acc"], 1)
            eng.tensor_copy(wxv_hi[:, :, :], raw_kv[:, 1, :, :]).then_inc(S["w_acc"], 1)
            eng.wait_ge(S["w_acc"], 11)
            for k, src in enumerate(order):
                if src is not None:
                    eng.tensor_tensor(w_lo[:, k, :, :], raw[:, src, :, :], w_hi[:, k, :, :], ALU.subtract)
            for k, src in ((1, 0), (3, 1)):
                pairs = raw[:, src, :, :].rearrange("p k (a b) -> p (k a) b", b=2)
                hi = w_hi[:, k, :, :].rearrange("p k (a b) -> p (k a) b", b=2)
                lo = w_lo[:, k, :, :].rearrange("p k (a b) -> p (k a) b", b=2)
                eng.scalar_tensor_tensor(out=lo[:, :, 0], in0=pairs[:, :, 1], scalar=-1.0, in1=hi[:, :, 0],
                                         op0=ALU.mult, op1=ALU.subtract)
                eng.tensor_tensor(lo[:, :, 1], pairs[:, :, 0], hi[:, :, 1], ALU.subtract)
            eng.tensor_tensor(kx_lo, kx_rep, kx_hi, ALU.subtract)
            eng.tensor_tensor(wxv_lo[:, :, :], raw_kv[:, 1, :, :], wxv_hi[:, :, :], ALU.subtract)\
               .then_inc(S["w_split"], 1)
            eng.wait_ge(S["w_abs_all"], 1)
            eng.tensor_scalar(thr[:, 0, :], bank[0][:, 0, 0:2], 0.7, None, ALU.mult).then_inc(S["w_thr"], 1)
            eng.wait_ge(S["w_thr"], 1)
            eng.tensor_scalar(thr[:, 1, :], thr[:, 0, :], -1.0, None, ALU.mult).then_inc(S["w_thr"], 1)
            eng.wait_ge(S["w_thr"], 2)
            for k, (r_, q_, s_) in enumerate((
                    (w1_raw, w1q[:, :, :].rearrange("p a b -> p (a b)"), "w_quant1"),
                    (w2_raw, w2q[:, :, :].rearrange("p a b -> p (a b)"), "w_quant2"))):
                if k:
                    eng.wait_ge(S["w_quant1"], 1)
                eng.tensor_scalar(w_scr, r_, thr[:, 1, k:k + 1], None, ALU.is_le).then_inc(S["w_ge"], 1)
                eng.wait_ge(S["w_ge"], k + 1)
                eng.scalar_tensor_tensor(out=q_, in0=r_, scalar=thr[:, 0, k:k + 1], in1=w_scr,
                                         op0=ALU.is_ge, op1=ALU.subtract).then_inc(S[s_], 1)
            eng.wait_ge(S["c_in"], 16 * 11)
            eng.wait_ge(S["w_zero"], 3)

            def low_part(o, k, hi, step):
                eng.tensor_tensor(o[:, :, :], bank[k][:, :, :], hi[:, :, :], ALU.subtract).then_inc(S[step], 1)

            def times_table(o, k, table, step):
                eng.tensor_tensor(o[:, :, :].rearrange("p k (s t) -> p (k s) t", t=SEQ),
                                  bank[k][:, :, :].rearrange("p k (s t) -> p (k s) t", t=SEQ),
                                  bcast(xpos[:, table, :], 1, KC * BS), ALU.mult).then_inc(S[step], 1)

            def layer_norm(k, psum_bank, residual, y, n, y_done):
                eng.tensor_tensor(y[:, :, :], psum_bank[:, :, :], residual[:, :, :], ALU.add)\
                   .then_inc(S[f"a{k}"], 1)
                done(eng, f"a{k}", n)
                for t in range(TP):
                    mm = eng.bn_stats(bn6[:, k - 1, t, :], y[:, t, :])
                mm.then_inc(S[f"st{k}"], 1)
                done(eng, f"st{k}", n)
                eng.memset(carrier[:, k:k + 1], 0.0)
                for t in range(TP):
                    mm = eng.bn_aggr(bn2[:, k - 1, t, :], bn6[:, k - 1, t, :])
                mm.then_inc(S[f"ag{k}"], 1)
                done(eng, f"po{k}", n)
                for t in range(TP):
                    mm = eng.tensor_scalar(y[:, t, :], y[:, t, :], bn2[:, k - 1, t, 0:1],
                                           rstd[:, k - 1, t:t + 1], ALU.subtract, ALU.mult)
                mm.then_inc(S[y_done], 1)

            def softmax_shift(t, b):
                done(eng, f"s{t}", b)
                rows = big[:, :, :, :].rearrange("p r c (j s) -> p (r c j) s", s=SEQ)
                eng.tensor_reduce(e_max[:, :], rows, AX.X, ALU.max).then_inc(S[f"m{t}"], 1)
                done(eng, f"m{t}", b)
                if t == 0:
                    done(eng, "t1", b, 1)
                else:
                    done(eng, "t0", b)
                eng.tensor_tensor(e_sb[:, :, :], rows, bcast(e_max[:, :], 2, SEQ), ALU.subtract)\
                   .then_inc(S[f"d{t}"], 1)

            def probs_out(t, b):
                done(eng, f"t{t}", b)
                if t == 0:
                    done(eng, "pv1", b, 1)
                else:
                    done(eng, "pv0", b)
                eng.tensor_copy(pT[:, 2:4, :, :, :].rearrange("p r a b c -> p (r a b c)"),
                                big[:, 2:4, :, :].rearrange("p r a b -> p (r a b)")).then_inc(S[f"p{t}b"], 1)

            def normalize(t, b):
                done(eng, f"pv{t}", b)
                den = bank[0][:, 1, :].rearrange("p (c s) -> p c s", c=KC)
                num = bank[0][:, 0, :].rearrange("p (c s) -> p c s", c=KC)
                done(eng, "o2", b, 1)
                eng.reciprocal(oT[:, t, :, :], den).then_inc(S[f"rd{t}"], 1)
                done(eng, f"rd{t}", b)
                eng.tensor_tensor(oT[:, t, :, :], num, oT[:, t, :, :], ALU.mult).then_inc(S[f"o{t}d"], 1)

            def decayed(t, i):
                done(eng, f"r{t}", i)
                done(eng, "av", i, 1)
                eng.tensor_tensor(rT[:, t, :, :, :, :].rearrange("p r c q s -> p (r c q s)"),
                                  big[:, :, :, :].rearrange("p r c s -> p (r c s)"), decay[:, :],
                                  ALU.mult).then_inc(S[f"rm{t}"], 1)

            def one(i, on):
                ret, gate, cross, ffn = on
                g, b, f = i - LAG_GATE, i - LAG_CROSS, i - LAG_FFN
                if ret:
                    done(eng, "xTh", i)
                    done(eng, "g", i, 1)
                    low_part(xT_lo, 0, xT_hi, "xTl")
                if gate:
                    done(eng, "cTh", g)
                    done(eng, "vx_ps", g, 1)
                    low_part(cT_lo, 1, cT_hi, "cTl")
                if cross:
                    done(eng, "x1Th", b)
                    done(eng, "xq", b, 1)
                    low_part(x1T_lo, 2, x1T_hi, "x1Tl")
                if ffn:
                    done(eng, "x2Th", f)
                    done(eng, "f3", f, 1)
                    low_part(x2T_lo, 3, x2T_hi, "x2Tl")
                if gate:
                    done(eng, "mu", g)
                    done(eng, "sqd", g, 1)
                    done(eng, "yn", g, 1)
                    eng.tensor_tensor(y_mid[:, :, :], y_sb[:, :, :], bank[0][:, :, :], ALU.subtract)\
                       .then_inc(S["ymid"], 1)
                if ret:
                    done(eng, "q", i)
                    done(eng, "qpar", i, 1)
                    times_table(q_cos, 1, 0, "qcos")
                    done(eng, "qr", i)
                    done(eng, "kadd", i, 1)
                    times_table(rot_sin, 2, 1, "qsin")
                if gate:
                    done(eng, "var", g)
                    done(eng, "ypow", g, 1)
                    eng.tensor_scalar(y_var[:, :], bank[0][:, 0, 0:TP * KC * 8], ATTN_EPS, None, ALU.add)\
                       .then_inc(S["veps"], 1)
                if ret:
                    done(eng, "k", i)
                    done(eng, "r1", i, 1)
                    done(eng, "kadd", i, 1)
                    times_table(k_all, 1, 2, "kcos")
                    done(eng, "kr", i)
                    done(eng, "qadd", i)
                    times_table(rot_sin, 2, 3, "ksin")
                if cross:
                    softmax_shift(0, b)
                if ret:
                    done(eng, "th", i)
                    eng.scalar_tensor_tensor(out=gate_th[:, :, :], in0=gate_th[:, :, :], scalar=1.0,
                                             in1=bank[1][:, :, :], op0=ALU.add, op1=ALU.mult)\
                       .then_inc(S["gp"], 1)
                if gate:
                    done(eng, "rt", g)
                    done(eng, "rx", g, 1)
                    eng.tensor_copy(y_rstdT[:, :], bank[2][0:32, 0, 0:P]).then_inc(S["rt_sb"], 1)
                if cross:
                    probs_out(0, b)
                if gate:
                    done(eng, "rx", g)
                    done(eng, "z", g, 1)
                    eng.tensor_tensor(y_norm[:, :, :], y_mid[:, :, :], bank[2][:, :, :], ALU.mult)\
                       .then_inc(S["yn"], 1)
                if cross:
                    softmax_shift(1, b)
                if gate:
                    done(eng, "kx_ps", g)
                    done(eng, "s1", g, 1)
                    for c in range(KC):
                        mm = eng.tensor_tensor(
                            kx[:, c, :, :, :],
                            bcast(bank[2][:, c, :].rearrange("p (s t) -> p s t", t=SEQ), 2, XJ),
                            bcast(bcast(small[:, 2:2 + XJ], 1, BS), 3, SEQ), ALU.mult)
                    mm.then_inc(S["kx_sb"], 1)
                if cross:
                    normalize(0, b)
                if gate:
                    done(eng, "yaff", g)
                    done(eng, "gmove", g)
                    done(eng, "o1", g, 1)
                    eng.tensor_tensor(zT[:, :, :], gate_sb[:, :, :], y_norm[:, :, :], ALU.mult)\
                       .then_inc(S["z"], 1)
                if ffn:
                    done(eng, "f_out", f)
                    done(eng, "x2b", f)
                    if not (isinstance(f, int) and f == 0):
                        eng.wait_ge(S["x_store"], 16 * f)
                    layer_norm(3, bank[1], x2_b, y_out, f, "y3d")
                if gate:
                    done(eng, "o1", g)
                    done(eng, "xres", g)
                    done(eng, "x1T", g, 1)
                    done(eng, "x1b", g, 1)
                    layer_norm(1, bank[2], x_res, x1, g, "x1d")
                if cross:
                    probs_out(1, b)
                if ret:
                    decayed(0, i)
                if cross:
                    normalize(1, b)
                    done(eng, "o2", b)
                    done(eng, "x1b", b)
                    done(eng, "x2T", b, 1)
                    done(eng, "x2b", b, 1)
                    layer_norm(2, bank[2], x1_b, x2, b, "x2d")
                if ret:
                    decayed(1, i)
            iterations(eng, one)

        @block.gpsimd
        def _(eng):
            eng.memset(all_mean[:, :], 1.0 / (F * D)).then_inc(S["w_zero"], 1)
            eng.memset(v_par[:, :, :, :].rearrange("p a b c -> p (a b c)"), 0.0).then_inc(S["w_zero"], 1)
            eng.memset(vx_bd[:, :, :, :, :].rearrange("p a b c d -> p (a b c d)"), 0.0)\
               .then_inc(S["w_zero"], 1)
            eng.dma_start(bfc_sb[:, :], xbfc.partition_broadcast(P)).then_inc(S["bias_in"], 16)
            eng.dma_start(b2_sb[:, :], b2.partition_broadcast(P)).then_inc(S["bias_in"], 16)
            eng.memset(minus_half[:, :], -0.5).then_inc(S["w_zero"], 1)

            def carry(place):
                eng.tensor_tensor(carrier[:, place:place + 1], minus_half[:, 0:1], minus_half[:, 0:1], ALU.add)

            def power(k, n):
                done(eng, f"ag{k}", n)
                done(eng, {1: "x1d", 2: "x2d", 3: "y3d"}[k], n, 1)
                carry(3 + k)
                eng.tensor_scalar(rstd[:, k - 1, :], bn2[:, k - 1, :, 1], EPS, None, ALU.add)\
                   .then_inc(S[f"ep{k}"], 1)
                done(eng, f"ep{k}", n)
                eng.tensor_tensor(rstd[:, k - 1, :], rstd[:, k - 1, :], minus_half[:, 0:TP], ALU.pow)\
                   .then_inc(S[f"po{k}"], 1)

            eng.wait_ge(S["w_zero"], 4)
            eng.wait_ge(S["bias_in"], 32)
            eng.wait_ge(S["c_in"], 16 * 11)

            def one(i, on):
                ret, gate, cross, ffn = on
                g, b, f = i - LAG_GATE, i - LAG_CROSS, i - LAG_FFN
                if cross:
                    done(eng, "x1d", b)
                    done(eng, "a2", b, 1)
                    for t in range(TP):
                        mm = eng.tensor_tensor(x1_b[:, t, :], x1[:, t, :], bfc_sb[:, :], ALU.add)
                    mm.then_inc(S["x1b"], 1)
                if ffn:
                    done(eng, "x2d", f)
                    done(eng, "a3", f, 1)
                    for t in range(TP):
                        mm = eng.tensor_tensor(x2_b[:, t, :], x2[:, t, :], b2_sb[:, :], ALU.add)
                    mm.then_inc(S["x2b"], 1)
                if ret:
                    done(eng, "qcos", i)
                    done(eng, "qsin", i)
                    eng.tensor_tensor(q_cos[:, :, :], q_cos[:, :, :], rot_sin[:, :, :], ALU.add)\
                       .then_inc(S["qadd"], 1)
                    done(eng, "qadd", i)
                    done(eng, "r1", i, 1)
                    carry(7)
                    for par in range(2):
                        mm = eng.tensor_scalar(q_par[:, par, :, :], q_cos[:, :, :], small[:, par:par + 1], None,
                                               ALU.mult)
                    mm.then_inc(S["qpar"], 1)
                if gate:
                    done(eng, "veps", g)
                    done(eng, "rt", g, 1)
                    eng.tensor_tensor(y_rstd[:, :], y_var[:, :], minus_half[:, :], ALU.pow)\
                       .then_inc(S["ypow"], 1)
                if ret:
                    done(eng, "kcos", i)
                    done(eng, "ksin", i)
                    done(eng, "r1", i, 1)
                    eng.tensor_tensor(k_all[:, :, :], k_all[:, :, :], rot_sin[:, :, :], ALU.add)\
                       .then_inc(S["kadd"], 1)
                if gate:
                    done(eng, "yn", g)
                    carry(8)
                    for kc in range(KC):
                        mm = eng.tensor_scalar(y_norm[:, kc, :], y_norm[:, kc, :], gn_w[:, kc:kc + 1],
                                               gn_b[:, kc:kc + 1], ALU.mult, ALU.add)
                    mm.then_inc(S["yaff"], 1)
                if ffn:
                    for u in range(4):
                        part = slice(2 * u, 2 * u + 2)
                        done(eng, f"h{u}", f)
                        done(eng, "f_out", f, 1)
                        carry(9 + u)
                        eng.tensor_scalar(h_hi[:, part, :], h_sb[:, part, :], 1.0, None, ALU.mult)\
                           .then_inc(S["h_hi"], 1)
                        eng.wait_ge(S["h_hi"], 4 * f + (u + 1))
                        eng.tensor_tensor(h_lo[:, part, :], h_sb[:, part, :], h_hi[:, part, :], ALU.subtract)\
                           .then_inc(S[f"hs{u}"], 1)
                if ret:
                    done(eng, "gp", i)
                    done(eng, "z", i, 1)
                    carry(13)
                    eng.tensor_scalar(gate_sb[:, :, :], gate_th[:, :, :], 0.5, None, ALU.mult)\
                       .then_inc(S["gmove"], 1)
                if ffn:
                    power(3, f)
                if gate:
                    power(1, g)
                if ret:
                    eng.wait_ge(S["x_load"], 16 * i + 16)
                    done(eng, "a1", i, 1)
                    carry(14)
                    eng.tensor_scalar(x_res[:, :, :], x_in[:, :, :], 1.0, None, ALU.mult).then_inc(S["xres"], 1)
                if cross:
                    power(2, b)
            iterations(eng, one)


_CONSTS = ("c_xpos", "c_decay", "c_small", "c_mats", "c_ones", "c_spread")


def kernel(x, ctx_2048, L0_attn_W_Q, L0_attn_W_K, L0_attn_W_V, L0_attn_W_G, L0_attn_W_O,
           L0_attn_gn_weight, L0_attn_gn_bias, L0_xattn_Wq, L0_xattn_Wk, L0_xattn_Wv, L0_xattn_Wfc,
           L0_xattn_bfc, L0_ffn_w1, L0_ffn_b1, L0_ffn_w2, L0_ffn_b2):
    import numpy as _np
    import concourse.bacc as _bacc
    from concourse import mybir as _mybir
    from concourse.bass_utils import run_bass_kernel_spmd as _run

    def heads(w):
        return _np.asarray(w).transpose(1, 0, 2).reshape(D, D)

    def columns(v):
        return _np.asarray(v).reshape(-1, P).T

    laid = {
        "x": _np.asarray(x).reshape(TOKENS, D), "ctx": _np.asarray(ctx_2048).reshape(TOKENS, D),
        "wq": heads(L0_attn_W_Q), "wk": heads(L0_attn_W_K), "wv": heads(L0_attn_W_V),
        "wg": _np.asarray(L0_attn_W_G), "wo": _np.asarray(L0_attn_W_O),
        "gnw": columns(L0_attn_gn_weight), "gnb": columns(L0_attn_gn_bias),
        "xwq": _np.asarray(L0_xattn_Wq).T, "xwk": _np.asarray(L0_xattn_Wk).T,
        "xwv": _np.asarray(L0_xattn_Wv).T, "xwfc": _np.asarray(L0_xattn_Wfc).T,
        "xbfc": _np.asarray(L0_xattn_bfc),
        "w1": _np.asarray(L0_ffn_w1).T, "b1": columns(L0_ffn_b1),
        "w2": _np.asarray(L0_ffn_w2).T, "b2": _np.asarray(L0_ffn_b2),
    }
    tables = shape_constants()
    laid.update({name: tables[name] for name in _CONSTS})
    nc = _bacc.Bacc("TRN2", target_bir_lowering=False, num_devices=1)
    arrays, args = {}, []
    for name, a in laid.items():
        a = _np.ascontiguousarray(a)
        arrays[f"in_{name}"] = a
        args.append(nc.dram_tensor(f"in_{name}", a.shape, _mybir.dt.from_np(a.dtype), kind="ExternalInput").ap())
    args.append(nc.dram_tensor("out_0", (TOKENS, D), F32, kind="ExternalOutput").ap())
    build(nc, *args)
    r = _run(nc, [arrays], core_ids=[0])
    return r.results[0]["out_0"].reshape(SEQS, SEQ, D)
```

```python
from contextlib import ExitStack

import numpy as np

import concourse.bass as bass
from concourse import mybir
from concourse.alu_op_type import AluOpType as ALU

F32 = mybir.dt.float32
F32R = mybir.dt.float32r
BF16 = mybir.dt.bfloat16
ACT = mybir.ActivationFunctionType
AX = mybir.AxisListType

SEQS, SEQ, D = 64, 64, 256
TOKENS = SEQS * SEQ
P = 128
KC = D // P
TB = 256
TP = TB // P
BS = TB // SEQ
NB = TOKENS // TB
HEADS, HD = 16, 16
HC = HEADS // KC
SPLITS = ((0, 0), (0, 1), (1, 0), (0, 2), (2, 0), (1, 1))
SROWS = len(SPLITS) * HD
XHEADS, XG, XD = 32, 8, 8
XJ = XHEADS // XG
F = 1024
FC = F // P
EPS = 1e-5
ATTN_EPS = 1e-5
LAG_GATE, LAG_CROSS, LAG_FFN = 1, 2, 3


def shape_constants():
    f = np.float32
    half = HD // 2
    xscale = (np.arange(0, HD, 2, dtype=f) + f(0.4 * HD)) / f(1.4 * HD)
    pos = np.arange(SEQ, dtype=f)
    scale = xscale[None, :] ** (pos[:, None] / f(64))
    inv = f(1.0) / f(10000.0) ** (np.arange(half, dtype=f) / f(half))
    angle = pos[:, None] * inv[None, :]
    p = np.arange(P)
    pair = (p % HD) // 2
    sign = np.where(p % 2 == 0, f(-1), f(1))[:, None]
    xpos = np.stack([(np.cos(angle) * scale)[:, pair].T, (np.cos(angle) * (f(1) / scale))[:, pair].T,
                     sign * (np.sin(angle) * scale)[:, pair].T,
                     sign * (np.sin(angle) * (f(1) / scale))[:, pair].T], 1).astype(f)
    gammas = f(1) - np.exp(np.linspace(np.log(1.0 / 32), np.log(1.0 / 64), HEADS)).astype(f)
    b, t = p // SEQ, p % SEQ
    decay = np.zeros((P, HC, KC, P), f)
    lag = (t[None, :] - t[:, None])
    seen = (b[None, :] == b[:, None]) & (lag >= 0)
    for h in range(HC):
        for c in range(KC):
            decay[:, h, c] = np.where(seen, gammas[HC * c + h] ** np.maximum(lag, 0).astype(f), 0)
    small = np.zeros((P, XJ + HC), f)
    for j in range(XJ):
        small[:, j] = (p % 32) // XD == j
    mats = np.zeros((P, 4, P), f)
    mats[:, 0] = np.eye(P)
    mats[:, 1] = (p[:, None] // HD == p[None, :] // HD) / HD
    for s in range(2):
        mats[:, 2 + s] = (b[:, None] == s) & (t[:, None] == t[None, :])
    ones = np.zeros((P, 2, 32), f)
    for jj in range(2):
        ones[:, jj] = np.arange(32)[None, :] // XD == 2 * jj + b[:, None]
    small[:, XJ:] = (p[:, None] // HD == np.arange(8)[None, :]) / HD
    spread = np.zeros((P, 4, P), f)
    for tc in range(4):
        for h in range(8):
            spread[8 * tc + h, tc] = p // HD == h
    return {"c_spread": spread.reshape(P, -1), "c_xpos": xpos, "c_decay": decay.reshape(P, -1), "c_small": small,
            "c_mats": mats.reshape(P, -1), "c_ones": ones.reshape(P, -1)}


def build(nc, x, ctx, wq, wk, wv, wg, wo, gnw, gnb, xwq, xwk, xwv, xwfc, xbfc, w1, b1, w2, b2,
          c_xpos, c_decay, c_small, c_mats, c_ones, c_spread, out):
    x_blocks = x.rearrange("(n t p) c -> n p t c", p=P, t=TP)
    ctx_blocks = ctx.rearrange("(n t p) c -> n p t c", p=P, t=TP)
    out_blocks = out.rearrange("(n t p) c -> n p t c", p=P, t=TP)

    scratch = nc.dram_tensor("qk_scratch", (NB, P, 3 * 2 * KC * TB), BF16, kind="Internal").ap()
    qk_blocks = scratch
    qk_heads = scratch.rearrange("n (h d) (a f) -> n d h a f", d=HD, f=KC * TB)

    stack = ExitStack()
    with stack:
        def sb(name, shape, dt=F32):
            return stack.enter_context(nc.sbuf_tensor(name, shape, dt))

        def ps(name, shape, dt=F32):
            return stack.enter_context(nc.psum_tensor(name, shape, dt))

        def sem(name):
            return stack.enter_context(nc.semaphore(name))

        NW = 6
        w_hi = sb("w_hi", [P, NW, KC, D], F32R)
        w_lo = sb("w_lo", [P, NW, KC, D], F32R)
        wxv_hi = sb("wxv_hi", [P, KC, XG * XD], F32R)
        wxv_lo = sb("wxv_lo", [P, KC, XG * XD], F32R)
        wo_sb = sb("wo_sb", [P, KC, D])
        wfc_sb = sb("wfc_sb", [P, KC, D])
        w1q = sb("w1q", [P, KC, F], F32R)
        w2q = sb("w2q", [P, FC, D], F32R)
        xpos = sb("xpos", [P, 4, SEQ])
        decay = sb("decay", [P, 2 * KC * 4 * P])
        small = sb("small", [P, XJ + HC])
        spread = sb("spread", [32, 4, P])
        mats = sb("mats", [P, 4, P])
        ones = sb("ones", [P, 2, 32])
        gn_w = sb("gn_w", [P, KC])
        gn_b = sb("gn_b", [P, KC])
        b1_sb = sb("b1_sb", [P, FC])
        bfc_sb = sb("bfc_sb", [P, D])
        b2_sb = sb("b2_sb", [P, D])
        all_mean = sb("all_mean", [P, P])
        abs_sum = sb("abs_sum", [P, 2])
        thr = sb("thr", [P, 2, 2])

        x_in = sb("x_in", [P, TP, D])
        ctx_in = sb("ctx_in", [P, TP, D])
        x_res = sb("x_res", [P, TP, D])
        xT_hi, xT_lo = sb("xT_hi", [P, KC, TB], F32R), sb("xT_lo", [P, KC, TB], F32R)
        cT_hi, cT_lo = sb("cT_hi", [P, KC, TB], F32R), sb("cT_lo", [P, KC, TB], F32R)
        x1T_hi, x1T_lo = sb("x1T_hi", [P, KC, TB], F32R), sb("x1T_lo", [P, KC, TB], F32R)
        x2T_hi, x2T_lo = sb("x2T_hi", [P, KC, TB], F32R), sb("x2T_lo", [P, KC, TB], F32R)
        qk = sb("qk", [P, 2, KC, TB])
        qk_swap = sb("qk_swap", [P, 2, KC, TB])
        qk_part = sb("qk_part", [P, 3, 2, KC, TB], BF16)
        qk_st = sb("qk_st", [SROWS, HC, 2, KC, TB], BF16)
        v_par = sb("v_par", [P, 2, TP, D])
        rT = sb("rT", [P, HC, KC, P])
        gate_th = sb("gate_th", [P, KC, TB])
        gate_sb = sb("gate_sb", [P, KC, TB])
        y_sb = sb("y_sb", [P, KC, TB])
        y_mid = sb("y_mid", [P, KC, TB])
        y_var = sb("y_var", [P, TP * KC * 8])
        y_rstd = sb("y_rstd", [P, TP * KC * 8])
        y_rstdT = sb("y_rstdT", [TP * KC * 8, P])
        y_norm = sb("y_norm", [P, KC, TB])
        y_sq = y_norm
        carrier = sb("carrier", [P, 16])
        minus_half = sb("minus_half", [P, TP * KC * 8])
        zT = sb("zT", [P, KC, TB])
        bn6 = sb("bn6", [P, 3, TP, 6])
        bn2 = sb("bn2", [P, 3, TP, 2])
        rstd = sb("rstd", [P, 3, TP])
        x1 = sb("x1", [P, TP, D])
        x1_b = sb("x1_b", [P, TP, D])
        x2 = sb("x2", [P, TP, D])
        x2_b = sb("x2_b", [P, TP, D])
        y_out = sb("y_out", [P, TP, D])
        qx = sb("qx", [P, KC, TB])
        kx = sb("kx", [P, KC, BS, XJ, SEQ])
        vx = sb("vx", [P, TP, XG * XD])
        vx_bd = sb("vx_bd", [P, 2 * TP, XG, 2, 32])
        e_sb = sb("e_sb", [P, XHEADS, SEQ])
        e_max = sb("e_max", [P, XHEADS])
        pT = sb("pT", [P, 4, KC, 2, P])
        oT = sb("oT", [P, TP, KC, P])
        h_sb = sb("h_sb", [P, 2, 2, TB])
        h_hi, h_lo = sb("h_hi", [P, FC, TB], F32R), sb("h_lo", [P, FC, TB], F32R)
        raw = rT[:, :, :, :].rearrange("p h c s -> p (h c s)")\
            .rearrange("p (w k n) -> p w k n", w=4, k=KC)
        raw_xq = ctx_in[:, :, :]
        raw_kv = y_sb[:, :, :].rearrange("p a b -> p (a b)")[:, 0:2 * KC * XG * XD]\
            .rearrange("p (w k n) -> p w k n", w=2, k=KC)
        w1_raw = e_sb[:, :, :].rearrange("p a b -> p (a b)")
        w2_raw = pT[:, :, :, :, :].rearrange("p a b c d -> p (a b c d)")

        bank = [ps(f"bank{k}", [P, 2, 256]) for k in range(4)]
        big = ps("big", [P, 4, 2, 256])

        names = """w_in wf_in c_in late_in bias_in w_split w_quant1 w_quant2 w_abs w_abs_all w_thr w_zero
            w_ge w_acc x_load c_load x_store qk_swapped qk_stored qk_stacked
            xT cT x1T x2T mu q xq var k s0 v g rt rx o1 f0 f1 f2 f3 t0 kx_ps vx_ps s1 pv0 f_out t1
            r0 pv1 vd o2 r1 av0 av
            q_ev k_ev qk_hi qk_mid qk_cos qk_sin qk_sum qk_rem qk_lo
            xTh cTh x1Th x2Th sqd qx_sb v_sb th e0 e1 h0 h1 h2 h3 p0a p1a vx_sb vbd y_ev
            xTl cTl x1Tl x2Tl ymid yn rt_sb veps m0 m1 d0 d1 z gp a1 st1 ag1 x1d
            p0b p1b kx_sb rd0 rd1 o0d o1d a3 st3 ag3 y3d rm0 rm1 a2 st2 ag2 x2d
            gmove x1b x2b ypow ep1 ep2 ep3 po1 po2 po3 yaff hh0 hh1 hh2 hh3 hs0 hs1 hs2 hs3 xres""".split()
        S = {n: sem(n) for n in names}
        block = stack.enter_context(nc.Block())

        def done(eng, name, i, lag=0):
            n = i - lag
            if isinstance(n, int):
                n = min(n, NB - 1)
                if n < 0:
                    return
            eng.wait_ge(S[name], n + 1)

        def freed(eng, i, *users):
            for name, lag in users:
                n = i - lag
                if not isinstance(n, int) or 0 <= n < NB:
                    eng.wait_ge(S[name], n + 1)
                    return

        def iterations(eng, one):
            def act(i):
                return [0 <= i - lag < NB for lag in range(4)]
            for i in range(LAG_FFN + 1):
                one(i, act(i))
            with eng.Fori(0, NB - (LAG_FFN + 1)) as j:
                one(j + (LAG_FFN + 1), [True] * 4)
            for i in range(NB, NB + LAG_FFN):
                one(i, act(i))

        ident = mats[:, 0, :]
        head_mean = mats[:, 1, :]

        @block.sync
        def _(eng):
            for k, w in enumerate((wq, wk, wv, wg)):
                eng.dma_start(raw[:, k, :, :], w.rearrange("(k p) n -> p k n", p=P)).then_inc(S["w_in"], 16)
            eng.dma_start(raw_xq, xwq.rearrange("(k p) n -> p k n", p=P)).then_inc(S["w_in"], 16)
            for k, w in enumerate((xwk, xwv)):
                eng.dma_start(raw_kv[:, k, :, :], w.rearrange("(k p) n -> p k n", p=P)).then_inc(S["w_in"], 16)

            def partners(src, par):
                return src[par:P:2, :, :, :]

            def one(i, on):
                ret, gate, cross, ffn = on
                if ret:
                    done(eng, "xT", i, 1)
                    done(eng, "xres", i, 1)
                    eng.dma_start(x_in[:, :, :], x_blocks[i, :, :, :]).then_inc(S["x_load"], 16)
                if isinstance(i, int) and i == 0:
                    for w_raw, w, k in ((w1_raw, w1, KC), (w2_raw, w2, FC)):
                        eng.dma_start(w_raw.rearrange("p (k n) -> p k n", k=k),
                                      w.rearrange("(k p) n -> p k n", p=P)).then_inc(S["wf_in"], 16)
                if gate:
                    n = i - LAG_GATE
                    if isinstance(n, int) and n == 0:
                        eng.wait_ge(S["w_split"], 1)
                    done(eng, "cT", n, 1)
                    eng.dma_start(ctx_in[:, :, :], ctx_blocks[n, :, :, :]).then_inc(S["c_load"], 16)
                if ret:
                    done(eng, "k_ev", i)
                    done(eng, "q_ev", i)
                    done(eng, "qk_lo", i, 1)
                    for par in range(2):
                        eng.dma_start(partners(qk_swap, par), partners(qk, 1 - par))\
                           .then_inc(S["qk_swapped"], 16)
                    done(eng, "qk_lo", i)
                    eng.dma_start(qk_blocks[i, :, :], qk_part[:, :, :, :, :].rearrange("p a w k t -> p (a w k t)"))\
                       .then_inc(S["qk_stored"], 16)
                    done(eng, "r1", i, 1)
                    eng.wait_ge(S["qk_stored"], 16 * i + 16)
                    for n, parts in enumerate(SPLITS):
                        rows = qk_st[n * HD:(n + 1) * HD, :, :, :, :].rearrange("d h w k t -> d h w (k t)")
                        for w in range(2):
                            eng.dma_start(rows[:, :, w, :], qk_heads[i, :, :, 2 * parts[w] + w, :])\
                               .then_inc(S["qk_stacked"], 16)
                if ffn:
                    n = i - LAG_FFN
                    done(eng, "y3d", n)
                    eng.dma_start(out_blocks[n, :, :, :], y_out[:, :, :]).then_inc(S["x_store"], 16)
            iterations(eng, one)
            eng.wait_ge(S["x_store"], 16 * NB)

        @block.tensor
        def _(eng):
            def flat(k):
                return bank[k][:, :, :].rearrange("p a b -> p (a b)")

            def transposes(src, k, step):
                for c in range(KC):
                    for t in range(TP):
                        mm = eng.transpose(bank[k][:, c, t * P:(t + 1) * P],
                                           src[:, t, c * P:(c + 1) * P], ident)
                mm.then_inc(S[step], 1)

            def split_product(o, parts, last, step=None):
                for n, (w, a) in enumerate(parts):
                    mm = eng.matmul(o, w, a, start=(n == 0), stop=(n == len(parts) - 1))
                if last:
                    mm.then_inc(S[step], 1)

            def project(w, hi, lo, k, step):
                for oc in range(KC):
                    cols = slice(oc * P, (oc + 1) * P)
                    parts = [(a[:, w, kc, cols], b[:, kc, :])
                             for a, b in ((w_lo, hi), (w_hi, lo), (w_hi, hi)) for kc in range(KC)]
                    split_product(bank[k][:, oc, :], parts, oc == KC - 1, step)

            def out_rows(act, w, k, step):
                for t in range(TP):
                    for kc in range(KC):
                        mm = eng.matmul(bank[k][:, t, :], act(t, kc), w[:, kc, :],
                                        start=(kc == 0), stop=(kc == KC - 1))
                mm.then_inc(S[step], 1)

            def ret_scores(t, step):
                scores = big[:, :, :, :].rearrange("p a b c -> p (a b c)")
                for h in range(HC):
                    for c in range(KC):
                        toks = slice(t * P, (t + 1) * P)
                        mm = eng.matmul(scores[:, (h * KC + c) * P:(h * KC + c + 1) * P],
                                        qk_st[:, h, 1, c, toks], qk_st[:, h, 0, c, toks],
                                        start=True, stop=True)
                mm.then_inc(S[step], 1)

            def ret_values(t, step):
                for c in range(KC):
                    for par in range(2):
                        for r in range(4):
                            mm = eng.matmul(bank[1][32 * r:32 * r + 32, c, t * P:(t + 1) * P],
                                            v_par[:, par, t, c * P + 32 * r:c * P + 32 * r + 32],
                                            rT[:, 2 * r + par, c, :],
                                            start=(par == 0), stop=(par == 1),
                                            tile_position=(0, 32 * r))
                mm.then_inc(S[step], 1)

            def cross_scores(t, step):
                for c in range(KC):
                    for r in range(4):
                        rows = slice(32 * r, 32 * r + 32)
                        for b in range(2):
                            tok = (2 * t + b) * SEQ
                            mm = eng.matmul(big[b * SEQ:(b + 1) * SEQ, r, c, :], qx[rows, c, tok:tok + SEQ],
                                            kx[rows, c, 2 * t + b, :, :].rearrange("p j s -> p (j s)"),
                                            start=True, stop=True)
                mm.then_inc(S[step], 1)

            def rstd_spread(g):
                done(eng, "rt_sb", g)
                for t in range(TP):
                    for c in range(KC):
                        mm = eng.matmul(bank[2][:, c, t * P:(t + 1) * P], spread[:, t * KC + c, :],
                                        y_rstdT[:, :], start=True, stop=True)
                mm.then_inc(S["rx"], 1)

            def prob_transposes(step):
                for r in range(4):
                    for q in range(4):
                        mm = eng.transpose(big[:, r, :, :].rearrange("p a b -> p (a b)")[:, q * P:(q + 1) * P],
                                           e_sb[:, :, :].rearrange("p h s -> p (h s)")
                                           [:, (4 * r + q) * P:(4 * r + q + 1) * P], ident)
                mm.then_inc(S[step], 1)

            def prob_values(t, k, step):
                for c in range(KC):
                    for b in range(2):
                        for jj in range(2):
                            for r in range(4):
                                eng.matmul(bank[k][32 * r:32 * r + 32, 0, c * P + b * SEQ:c * P + (b + 1) * SEQ],
                                           vx_bd[:, b * TP + t, 4 * c + r, jj, :],
                                           pT[:, r, c, jj, b * SEQ:(b + 1) * SEQ],
                                           start=(jj == 0), stop=(jj == 1), tile_position=(0, 32 * r))
                    for jj in range(2):
                        for r in range(4):
                            mm = eng.matmul(bank[k][32 * r:32 * r + 32, 1, c * P:(c + 1) * P],
                                            ones[:, jj, :], pT[:, r, c, jj, :],
                                            start=(jj == 0), stop=(jj == 1), tile_position=(0, 32 * r))
                mm.then_inc(S[step], 1)

            eng.wait_ge(S["c_in"], 16 * 3)

            def one(i, on):
                ret, gate, cross, ffn = on
                g, b, f = i - LAG_GATE, i - LAG_CROSS, i - LAG_FFN

                def feed_forward(u, k):
                    for oc in range(2):
                        fc = 2 * u + oc
                        parts = [(w1q[:, kc, fc * P:(fc + 1) * P], a[:, kc, :])
                                 for a in (x2T_lo, x2T_hi) for kc in range(KC)]
                        split_product(bank[k][:, oc, :], parts, oc == 1, f"f{u}")

                if isinstance(i, int) and i == 1:
                    eng.wait_ge(S["late_in"], 16 * 8)
                    eng.wait_ge(S["w_zero"], 3)
                    eng.wait_ge(S["w_abs"], 2)
                    done(eng, "v_sb", 0)
                    eng.matmul(bank[0][:, 0, 0:2], all_mean[:, :], abs_sum[:, :], start=True, stop=True)\
                       .then_inc(S["w_abs_all"], 1)
                    eng.wait_ge(S["w_thr"], 1)
                if ret:
                    eng.wait_ge(S["x_load"], 16 * i + 16)
                    freed(eng, i, ("o1d", 3), ("h1", 4), ("v_sb", 1))
                    transposes(x_in, 0, "xT")
                if gate:
                    eng.wait_ge(S["c_load"], 16 * g + 16)
                    freed(eng, i, ("y_ev", 1), ("a3", 4))
                    transposes(ctx_in, 1, "cT")
                if cross:
                    done(eng, "x1d", b)
                    freed(eng, i, ("a2", 3), ("a1", 2))
                    transposes(x1, 2, "x1T")
                if ret:
                    done(eng, "xTl", i)
                    if isinstance(i, int) and i == 0:
                        eng.wait_ge(S["w_split"], 1)
                    freed(eng, i, ("cTl", 1), ("y_ev", 1))
                    project(0, xT_hi, xT_lo, 1, "q")
                if gate:
                    done(eng, "y_ev", g)
                    freed(eng, i, ("xTl", 0), ("o1d", 3), ("h1", 4), ("v_sb", 1))
                    eng.matmul(flat(0), head_mean, y_sb[:, :, :].rearrange("p a b -> p (a b)"),
                               start=True, stop=True).then_inc(S["mu"], 1)
                if ret:
                    freed(eng, i, ("x1Tl", 2), ("a1", 2), ("k_ev", 1))
                    project(1, xT_hi, xT_lo, 2, "k")
                if ffn:
                    done(eng, "x2d", f)
                    freed(eng, i, ("vbd", 2), ("h2", 4))
                    transposes(x2, 3, "x2T")
                if gate:
                    done(eng, "sqd", g)
                    done(eng, "ymid", g)
                    for t in range(TP):
                        for c in range(KC):
                            mm = eng.matmul(bank[0][:, 0, (t * KC + c) * 8:(t * KC + c + 1) * 8],
                                            y_sq[:, c, t * P:(t + 1) * P], small[:, XJ:],
                                            start=True, stop=True)
                    mm.then_inc(S["var"], 1)
                if cross:
                    done(eng, "x1Tl", b)
                    freed(eng, i, ("x2Tl", 3), ("vbd", 2))
                    project(4, x1T_hi, x1T_lo, 3, "xq")
                if ret:
                    done(eng, "q_ev", i)
                    project(3, xT_hi, xT_lo, 1, "g")
                if cross:
                    done(eng, "qx_sb", b)
                    done(eng, "kx_sb", b)
                    freed(eng, i, ("rm1", 1), ("p1b", 3))
                    cross_scores(0, "s0")
                if ret:
                    freed(eng, i, ("veps", 1), ("xTl", 0))
                    for t in range(TP):
                        parts = [(a[:, kc, t * P:(t + 1) * P], w[:, 2, kc, :])
                                 for a, w in ((xT_lo, w_hi), (xT_hi, w_lo), (xT_hi, w_hi))
                                 for kc in range(KC)]
                        split_product(bank[0][:, t, :], parts, t == TP - 1, "v")
                if gate:
                    done(eng, "ypow", g)
                    freed(eng, i, ("k_ev", 0), ("x1Tl", 2), ("a1", 2))
                    eng.transpose(bank[2][0:32, 0, 0:P], y_rstd[:, :], ident).then_inc(S["rt"], 1)
                if ffn:
                    if isinstance(f, int) and f == 0:
                        eng.wait_ge(S["w_quant2"], 1)
                    done(eng, "x2Tl", f)
                    freed(eng, i, ("qx_sb", 2), ("x2Tl", 3))
                    feed_forward(0, 3)
                    freed(eng, i, ("v_sb", 0), ("veps", 1), ("o1d", 3))
                    feed_forward(1, 0)
                if gate:
                    rstd_spread(g)
                if cross:
                    done(eng, "e0", b)
                    done(eng, "d0", b)
                    prob_transposes("t0")
                if gate:
                    done(eng, "cTl", g)
                    done(eng, "yn", g)
                    project(5, cT_hi, cT_lo, 2, "kx_ps")
                if ffn:
                    freed(eng, i, ("h0", 3))
                    feed_forward(2, 3)
                    freed(eng, i, ("gp", 0), ("cTl", 1), ("a3", 4))
                    feed_forward(3, 1)
                if cross:
                    done(eng, "p0a", b)
                    done(eng, "p0b", b)
                    cross_scores(1, "s1")
                if gate:
                    freed(eng, i, ("h2", 3), ("qx_sb", 2), ("vbd", 2))
                    for t in range(TP):
                        parts = [(a[:, kc, t * P:(t + 1) * P], w[:, kc, :])
                                 for a, w in ((cT_lo, wxv_hi), (cT_hi, wxv_lo), (cT_hi, wxv_hi))
                                 for kc in range(KC)]
                        split_product(bank[3][:, 0, t * 64:(t + 1) * 64], parts, t == TP - 1, "vx_ps")
                if cross:
                    freed(eng, i, ("h1", 3), ("v_sb", 0), ("veps", 1), ("o1d", 3))
                    done(eng, "vbd", b)
                    prob_values(0, 0, "pv0")
                if gate:
                    done(eng, "z", g)
                    done(eng, "kx_sb", g)
                    out_rows(lambda t, kc: zT[:, kc, t * P:(t + 1) * P], wo_sb, 2, "o1")
                if cross:
                    done(eng, "e1", b)
                    done(eng, "d1", b)
                    prob_transposes("t1")
                if ffn:
                    freed(eng, i, ("h3", 3))
                    for t in range(TP):
                        n = 0
                        for fc in range(FC):
                            if t == 0 and fc % 2 == 0:
                                done(eng, f"hs{fc // 2}", f)
                            for a in (h_lo, h_hi):
                                mm = eng.matmul(bank[1][:, t, :], a[:, fc, t * P:(t + 1) * P], w2q[:, fc, :],
                                                start=(n == 0), stop=(n == 2 * FC - 1))
                                n += 1
                    mm.then_inc(S["f_out"], 1)
                if ret:
                    eng.wait_ge(S["qk_stacked"], 16 * 2 * len(SPLITS) * (i + 1))
                    freed(eng, i, ("p1b", 2), ("rm1", 1))
                    if not (isinstance(i, int) and not cross):
                        done(eng, "p1a", b)
                    ret_scores(0, "r0")
                if cross:
                    done(eng, "p1a", b)
                    done(eng, "p1b", b)
                    done(eng, "o0d", b)
                    prob_values(1, 0, "pv1")
                if ret:
                    done(eng, "rm0", i)
                    ret_scores(1, "r1")
                if gate:
                    done(eng, "vx_sb", g)
                    for s in range(2):
                        mm = eng.matmul(bank[3][:, 1, s * P:(s + 1) * P], mats[:, 2 + s, :],
                                        vx[:, :, :].rearrange("p t c -> p (t c)"), start=True, stop=True)
                    mm.then_inc(S["vd"], 1)
                if ret:
                    freed(eng, i, ("a3", 3), ("gp", 0))
                    ret_values(0, "av0")
                if cross:
                    done(eng, "o1d", b)
                    freed(eng, i, ("a1", 1), ("x1Tl", 2))
                    out_rows(lambda t, kc: oT[:, t, kc, :], wfc_sb, 2, "o2")
                if ret:
                    done(eng, "rm1", i)
                    ret_values(1, "av")
            iterations(eng, one)

        @block.scalar
        def _(eng):
            def copy(o, a):
                return eng.activation(o, a, ACT.Copy)

            eng.dma_start(mats[:, :, :].rearrange("p a b -> p (a b)"), c_mats).then_inc(S["c_in"], 16)
            eng.dma_start(small[:, :], c_small).then_inc(S["c_in"], 16)
            eng.dma_start(xpos[:, :, :].rearrange("p a b -> p (a b)"),
                          c_xpos.rearrange("p a b -> p (a b)")).then_inc(S["c_in"], 16)
            eng.dma_start(decay[:, :], c_decay).then_inc(S["late_in"], 16)
            eng.dma_start(spread[:, :, :].rearrange("p a b -> p (a b)"), c_spread[0:32, :])\
               .then_inc(S["late_in"], 16)
            eng.dma_start(ones[:, :, :].rearrange("p a b -> p (a b)"), c_ones).then_inc(S["late_in"], 16)
            eng.dma_start(wo_sb[:, :, :], wo.rearrange("(k p) n -> p k n", p=P)).then_inc(S["late_in"], 16)
            eng.dma_start(wfc_sb[:, :, :], xwfc.rearrange("(k p) n -> p k n", p=P)).then_inc(S["late_in"], 16)
            eng.dma_start(b1_sb[:, :], b1).then_inc(S["late_in"], 16)
            eng.dma_start(gn_w[:, :], gnw).then_inc(S["late_in"], 16)
            eng.dma_start(gn_b[:, :], gnb).then_inc(S["late_in"], 16)

            def one(i, on):
                ret, gate, cross, ffn = on
                g, b, f = i - LAG_GATE, i - LAG_CROSS, i - LAG_FFN

                def gelu(u, k):
                    done(eng, f"f{u}", f)
                    if u < 2:
                        done(eng, f"hs{u + 2}", f, 1)
                    else:
                        done(eng, f"hs{u - 2}", f)
                    for oc in range(2):
                        fc = 2 * u + oc
                        mm = eng.activation(h_sb[:, u % 2, oc, :], bank[k][:, oc, :], ACT.Gelu,
                                            bias=b1_sb[:, fc:fc + 1])
                    mm.then_inc(S[f"h{u}"], 1)
                    done(eng, f"h{u}", f)
                    done(eng, "f_out", f, 1)
                    copy(h_hi[:, 2 * u:2 * u + 2, :], h_sb[:, u % 2, :, :]).then_inc(S[f"hh{u}"], 1)

                if ret:
                    done(eng, "xT", i)
                    done(eng, "g", i, 1)
                    done(eng, "v", i, 1)
                    copy(xT_hi[:, :, :], bank[0][:, :, :]).then_inc(S["xTh"], 1)
                if gate:
                    done(eng, "cT", g)
                    done(eng, "vx_ps", g, 1)
                    copy(cT_hi[:, :, :], bank[1][:, :, :]).then_inc(S["cTh"], 1)
                if cross:
                    done(eng, "x1T", b)
                    done(eng, "xq", b, 1)
                    copy(x1T_hi[:, :, :], bank[2][:, :, :]).then_inc(S["x1Th"], 1)
                if ret:
                    done(eng, "q", i)
                    done(eng, "qk_rem", i, 1)
                    copy(qk[:, 0, :, :], bank[1][:, :, :]).then_inc(S["q_ev"], 1)
                if gate:
                    done(eng, "ymid", g)
                    done(eng, "var", g, 1)
                    eng.activation(y_sq[:, :, :], y_mid[:, :, :], ACT.Square).then_inc(S["sqd"], 1)
                if ret:
                    done(eng, "k", i)
                    copy(qk[:, 1, :, :], bank[2][:, :, :]).then_inc(S["k_ev"], 1)
                if ffn:
                    done(eng, "x2T", f)
                    done(eng, "f3", f, 1)
                    copy(x2T_hi[:, :, :], bank[3][:, :, :]).then_inc(S["x2Th"], 1)
                if cross:
                    done(eng, "xq", b)
                    done(eng, "s1", b, 1)
                    copy(qx[:, :, :], bank[3][:, :, :]).then_inc(S["qx_sb"], 1)
                if ret:
                    done(eng, "g", i)
                    done(eng, "gmove", i, 1)
                    eng.activation(gate_th[:, :, :], bank[1][:, :, :], ACT.Tanh, scale=0.5)\
                       .then_inc(S["th"], 1)
                    done(eng, "v", i)
                    done(eng, "av", i, 1)
                    if isinstance(i, int) and i == 0:
                        eng.wait_ge(S["w_zero"], 3)
                    for par in range(2):
                        cols = [t_[:, :, :].rearrange("p t (h c) -> p (t h) c", c=2 * HD)[:, :, par * HD:par * HD + HD]
                                for t_ in (v_par[:, par, :, :], bank[0][:, :, :])]
                        mm = copy(cols[0], cols[1])
                    mm.then_inc(S["v_sb"], 1)
                    done(eng, "qk_sum", i)
                    if not (isinstance(i, int) and i == 0):
                        eng.wait_ge(S["qk_stored"], 16 * i)
                    copy(qk_part[:, 0, :, :, :], qk[:, :, :, :]).then_inc(S["qk_hi"], 1)
                if cross:
                    done(eng, "d0", b)
                    eng.activation(e_sb[:, :, :], e_sb[:, :, :], ACT.Exp, scale=float(XD) ** -0.5)\
                       .then_inc(S["e0"], 1)
                if ret:
                    done(eng, "qk_rem", i)
                    copy(qk_part[:, 1, :, :, :], qk_swap[:, :, :, :]).then_inc(S["qk_mid"], 1)
                if ffn:
                    if isinstance(f, int) and f == 0:
                        eng.wait_ge(S["late_in"], 16 * 8)
                    gelu(0, 3)
                if cross:
                    done(eng, "t0", b)
                    done(eng, "pv1", b, 1)
                    copy(pT[:, 0:2, :, :, :].rearrange("p r a b c -> p (r a b c)"),
                         big[:, 0:2, :, :].rearrange("p r a b -> p (r a b)")).then_inc(S["p0a"], 1)
                if ffn:
                    gelu(1, 0)
                    gelu(2, 3)
                    gelu(3, 1)
                if gate:
                    done(eng, "vx_ps", g)
                    done(eng, "vd", g, 1)
                    copy(vx[:, :, :].rearrange("p t c -> p (t c)"), bank[3][:, 0, 0:P]).then_inc(S["vx_sb"], 1)
                if cross:
                    done(eng, "d1", b)
                    eng.activation(e_sb[:, :, :], e_sb[:, :, :], ACT.Exp, scale=float(XD) ** -0.5)\
                       .then_inc(S["e1"], 1)
                if cross:
                    done(eng, "t1", b)
                    done(eng, "pv0", b)
                    copy(pT[:, 0:2, :, :, :].rearrange("p r a b c -> p (r a b c)"),
                         big[:, 0:2, :, :].rearrange("p r a b -> p (r a b)")).then_inc(S["p1a"], 1)
                if ret:
                    done(eng, "gp", i)
                    done(eng, "z", i, 1)
                    eng.activation(gate_sb[:, :, :], gate_th[:, :, :], ACT.Copy, scale=0.5).then_inc(S["gmove"], 1)
                    eng.wait_ge(S["x_load"], 16 * i + 16)
                    done(eng, "a1", i, 1)
                    copy(x_res[:, :, :], x_in[:, :, :]).then_inc(S["xres"], 1)
                if gate:
                    done(eng, "vd", g)
                    done(eng, "pv1", g, 1)
                    for h in range(2):
                        rows = slice(h * SEQ, (h + 1) * SEQ)
                        src = bank[3][rows, 1, :].rearrange("p (a d) -> p a d", d=XD)
                        for jj in range(2):
                            mm = copy(vx_bd[rows, :, :, jj, (2 * jj + h) * XD:(2 * jj + h + 1) * XD]
                                      .rearrange("p a g d -> p (a g) d"), src)
                    mm.then_inc(S["vbd"], 1)
                if ret:
                    done(eng, "av", i)
                    done(eng, "ymid", i, 1)
                    copy(y_sb[:, :, :], bank[1][:, :, :]).then_inc(S["y_ev"], 1)
            iterations(eng, one)

        @block.vector
        def _(eng):
            def bcast(ap, axis, n):
                a = ap.unsqueeze(axis)
                shape = list(a.shape)
                shape[axis] = n
                return a.to_broadcast(shape)

            eng.wait_ge(S["w_in"], 16 * 7)
            sources = [raw[:, k, :, :] for k in range(4)] + [raw_xq]
            for k, src in enumerate(sources):
                eng.tensor_copy(w_hi[:, k, :, :], src).then_inc(S["w_acc"], 1)
            kx_rep = bcast(raw_kv[:, 0, :, :].rearrange("p k (g d) -> p (k g) d", d=XD), 2, XJ)
            kx_hi = w_hi[:, 5, :, :].rearrange("p k (g j d) -> p (k g) j d", j=XJ, d=XD)
            kx_lo = w_lo[:, 5, :, :].rearrange("p k (g j d) -> p (k g) j d", j=XJ, d=XD)
            eng.tensor_copy(kx_hi, kx_rep).then_inc(S["w_acc"], 1)
            eng.tensor_copy(wxv_hi[:, :, :], raw_kv[:, 1, :, :]).then_inc(S["w_acc"], 1)
            eng.wait_ge(S["w_acc"], 7)
            for k, src in enumerate(sources):
                eng.tensor_tensor(w_lo[:, k, :, :], src, w_hi[:, k, :, :], ALU.subtract)
            eng.tensor_tensor(kx_lo, kx_rep, kx_hi, ALU.subtract)
            eng.tensor_tensor(wxv_lo[:, :, :], raw_kv[:, 1, :, :], wxv_hi[:, :, :], ALU.subtract)\
               .then_inc(S["w_split"], 1)

            def weight_sums():
                eng.wait_ge(S["wf_in"], 16 * 2)
                for k, r_ in enumerate((w1_raw, w2_raw)):
                    eng.tensor_reduce(abs_sum[:, k:k + 1], r_, AX.X, ALU.add, apply_absolute_value=True)\
                       .then_inc(S["w_abs"], 1)

            def thresholds():
                eng.wait_ge(S["w_abs_all"], 1)
                eng.tensor_scalar(thr[:, 0, :], bank[0][:, 0, 0:2], 0.7, None, ALU.mult).then_inc(S["w_thr"], 1)
                eng.wait_ge(S["w_thr"], 1)
                eng.tensor_scalar(thr[:, 1, :], thr[:, 0, :], -1.0, None, ALU.mult).then_inc(S["w_thr"], 1)

            def ternary():
                eng.wait_ge(S["w_thr"], 2)
                for k, (r_, q_, s_) in enumerate((
                        (w1_raw, w1q[:, :, :].rearrange("p a b -> p (a b)"), "w_quant1"),
                        (w2_raw, w2q[:, :, :].rearrange("p a b -> p (a b)"), "w_quant2"))):
                    eng.tensor_scalar(q_, r_, thr[:, 1, k:k + 1], None, ALU.is_le).then_inc(S["w_ge"], 1)
                    eng.wait_ge(S["w_ge"], k + 1)
                    eng.scalar_tensor_tensor(out=q_, in0=r_, scalar=thr[:, 0, k:k + 1], in1=q_,
                                             op0=ALU.is_ge, op1=ALU.subtract).then_inc(S[s_], 1)

            def low_part(o, k, hi, step):
                eng.tensor_tensor(o[:, :, :], bank[k][:, :, :], hi[:, :, :], ALU.subtract).then_inc(S[step], 1)

            def times_tables(a, first, step):
                for w in range(2):
                    rows = a[:, w, :, :].rearrange("p k (s t) -> p (k s) t", t=SEQ)
                    mm = eng.tensor_tensor(rows, rows, bcast(xpos[:, first + w, :], 1, KC * BS), ALU.mult)
                mm.then_inc(S[step], 1)

            def norm_stats(k, psum_bank, residual, y, n):
                eng.tensor_tensor(y[:, :, :], psum_bank[:, :, :], residual[:, :, :], ALU.add)\
                   .then_inc(S[f"a{k}"], 1)
                done(eng, f"a{k}", n)
                for t in range(TP):
                    mm = eng.bn_stats(bn6[:, k - 1, t, :], y[:, t, :])
                mm.then_inc(S[f"st{k}"], 1)
                done(eng, f"st{k}", n)
                eng.memset(carrier[:, k:k + 1], 0.0)
                for t in range(TP):
                    mm = eng.bn_aggr(bn2[:, k - 1, t, :], bn6[:, k - 1, t, :])
                mm.then_inc(S[f"ag{k}"], 1)

            def norm_apply(k, y, n, y_done):
                done(eng, f"po{k}", n)
                for t in range(TP):
                    mm = eng.tensor_scalar(y[:, t, :], y[:, t, :], bn2[:, k - 1, t, 0:1],
                                           rstd[:, k - 1, t:t + 1], ALU.subtract, ALU.mult)
                mm.then_inc(S[y_done], 1)

            def softmax_shift(t, b):
                done(eng, f"s{t}", b)
                rows = big[:, :, :, :].rearrange("p r c (j s) -> p (r c j) s", s=SEQ)
                eng.tensor_reduce(e_max[:, :], rows, AX.X, ALU.max).then_inc(S[f"m{t}"], 1)
                done(eng, f"m{t}", b)
                if t == 0:
                    done(eng, "t1", b, 1)
                else:
                    done(eng, "t0", b)
                eng.tensor_tensor(e_sb[:, :, :], rows, bcast(e_max[:, :], 2, SEQ), ALU.subtract)\
                   .then_inc(S[f"d{t}"], 1)

            def probs_out(t, b):
                done(eng, f"t{t}", b)
                if t == 0:
                    done(eng, "pv1", b, 1)
                else:
                    done(eng, "pv0", b)
                eng.tensor_copy(pT[:, 2:4, :, :, :].rearrange("p r a b c -> p (r a b c)"),
                                big[:, 2:4, :, :].rearrange("p r a b -> p (r a b)")).then_inc(S[f"p{t}b"], 1)

            def normalize(t, b):
                done(eng, f"pv{t}", b)
                den = bank[0][:, 1, :].rearrange("p (c s) -> p c s", c=KC)
                num = bank[0][:, 0, :].rearrange("p (c s) -> p c s", c=KC)
                done(eng, "o2", b, 1)
                eng.reciprocal(oT[:, t, :, :], den).then_inc(S[f"rd{t}"], 1)
                done(eng, f"rd{t}", b)
                eng.tensor_tensor(oT[:, t, :, :], num, oT[:, t, :, :], ALU.mult).then_inc(S[f"o{t}d"], 1)

            def decayed(t, i):
                done(eng, f"r{t}", i)
                if t == 0:
                    done(eng, "av", i, 1)
                else:
                    done(eng, "av0", i)
                eng.tensor_tensor(rT[:, :, :, :].rearrange("p h c s -> p (h c s)"),
                                  big[:, :, :, :].rearrange("p r c s -> p (r c s)"), decay[:, :],
                                  ALU.mult).then_inc(S[f"rm{t}"], 1)

            def one(i, on):
                ret, gate, cross, ffn = on
                g, b, f = i - LAG_GATE, i - LAG_CROSS, i - LAG_FFN
                if isinstance(i, int) and i == 1:
                    thresholds()
                if isinstance(i, int) and i == 2:
                    ternary()
                if ret:
                    done(eng, "xTh", i)
                    done(eng, "g", i, 1)
                    done(eng, "v", i, 1)
                    low_part(xT_lo, 0, xT_hi, "xTl")
                if gate:
                    done(eng, "cTh", g)
                    done(eng, "vx_ps", g, 1)
                    low_part(cT_lo, 1, cT_hi, "cTl")
                if cross:
                    done(eng, "x1Th", b)
                    done(eng, "xq", b, 1)
                    low_part(x1T_lo, 2, x1T_hi, "x1Tl")
                if gate:
                    done(eng, "mu", g)
                    done(eng, "sqd", g, 1)
                    done(eng, "yn", g, 1)
                    eng.tensor_tensor(y_mid[:, :, :], y_sb[:, :, :], bank[0][:, :, :], ALU.subtract)\
                       .then_inc(S["ymid"], 1)
                if ffn:
                    done(eng, "x2Th", f)
                    done(eng, "f3", f, 1)
                    low_part(x2T_lo, 3, x2T_hi, "x2Tl")
                if gate:
                    done(eng, "var", g)
                    done(eng, "ypow", g, 1)
                    eng.tensor_scalar(y_var[:, :], bank[0][:, 0, 0:TP * KC * 8], ATTN_EPS, None, ALU.add)\
                       .then_inc(S["veps"], 1)
                if ret:
                    if isinstance(i, int) and i == 0:
                        eng.wait_ge(S["c_in"], 16 * 3)
                    eng.wait_ge(S["qk_swapped"], 32 * i + 32)
                    times_tables(qk, 0, "qk_cos")
                    times_tables(qk_swap, 2, "qk_sin")
                    done(eng, "qk_cos", i)
                    done(eng, "qk_sin", i)
                    eng.tensor_tensor(qk[:, :, :, :], qk[:, :, :, :], qk_swap[:, :, :, :], ALU.add)\
                       .then_inc(S["qk_sum"], 1)
                if cross:
                    softmax_shift(0, b)
                if gate:
                    done(eng, "rt", g)
                    done(eng, "rx", g, 1)
                    eng.tensor_copy(y_rstdT[:, :], bank[2][0:32, 0, 0:P]).then_inc(S["rt_sb"], 1)
                if ret:
                    done(eng, "th", i)
                    eng.scalar_tensor_tensor(out=gate_th[:, :, :], in0=gate_th[:, :, :], scalar=1.0,
                                             in1=bank[1][:, :, :], op0=ALU.add, op1=ALU.mult)\
                       .then_inc(S["gp"], 1)
                    done(eng, "qk_hi", i)
                    eng.tensor_tensor(qk_swap[:, :, :, :], qk[:, :, :, :], qk_part[:, 0, :, :, :],
                                      ALU.subtract).then_inc(S["qk_rem"], 1)
                if gate:
                    done(eng, "rx", g)
                    done(eng, "z", g, 1)
                    eng.tensor_tensor(y_norm[:, :, :], y_mid[:, :, :], bank[2][:, :, :], ALU.mult)\
                       .then_inc(S["yn"], 1)
                if cross:
                    probs_out(0, b)
                if gate:
                    done(eng, "kx_ps", g)
                    done(eng, "s1", g, 1)
                    for c in range(KC):
                        mm = eng.tensor_tensor(
                            kx[:, c, :, :, :],
                            bcast(bank[2][:, c, :].rearrange("p (s t) -> p s t", t=SEQ), 2, XJ),
                            bcast(bcast(small[:, 0:XJ], 1, BS), 3, SEQ), ALU.mult)
                    mm.then_inc(S["kx_sb"], 1)
                if cross:
                    softmax_shift(1, b)
                if gate:
                    done(eng, "yaff", g)
                    done(eng, "gmove", g)
                    done(eng, "o1", g, 1)
                    eng.tensor_tensor(zT[:, :, :], gate_sb[:, :, :], y_norm[:, :, :], ALU.mult)\
                       .then_inc(S["z"], 1)
                if cross:
                    normalize(0, b)
                if gate:
                    done(eng, "o1", g)
                    done(eng, "xres", g)
                    done(eng, "x1T", g, 1)
                    done(eng, "x1b", g, 1)
                    norm_stats(1, bank[2], x_res, x1, g)
                if cross:
                    probs_out(1, b)
                if gate:
                    norm_apply(1, x1, g, "x1d")
                if ffn:
                    done(eng, "f_out", f)
                    done(eng, "x2b", f)
                    if not (isinstance(f, int) and f == 0):
                        eng.wait_ge(S["x_store"], 16 * f)
                    norm_stats(3, bank[1], x2_b, y_out, f)
                if ret:
                    if isinstance(i, int) and i == 0:
                        eng.wait_ge(S["late_in"], 16 * 8)
                    decayed(0, i)
                if ffn:
                    norm_apply(3, y_out, f, "y3d")
                if cross:
                    normalize(1, b)
                if ret:
                    decayed(1, i)
                if cross:
                    done(eng, "o2", b)
                    done(eng, "x1b", b)
                    done(eng, "x2T", b, 1)
                    done(eng, "x2b", b, 1)
                    norm_stats(2, bank[2], x1_b, x2, b)
                    norm_apply(2, x2, b, "x2d")
                if isinstance(i, int) and i == 0:
                    weight_sums()
            iterations(eng, one)

        @block.gpsimd
        def _(eng):
            eng.memset(all_mean[:, :], 1.0 / (F * D)).then_inc(S["w_zero"], 1)
            eng.memset(v_par[:, :, :, :].rearrange("p a b c -> p (a b c)"), 0.0).then_inc(S["w_zero"], 1)
            eng.memset(vx_bd[:, :, :, :, :].rearrange("p a b c d -> p (a b c d)"), 0.0)\
               .then_inc(S["w_zero"], 1)
            eng.dma_start(bfc_sb[:, :], xbfc.partition_broadcast(P)).then_inc(S["bias_in"], 16)
            eng.dma_start(b2_sb[:, :], b2.partition_broadcast(P)).then_inc(S["bias_in"], 16)
            eng.memset(minus_half[:, :], -0.5).then_inc(S["w_zero"], 1)

            def carry(place):
                eng.tensor_tensor(carrier[:, place:place + 1], minus_half[:, 0:1], minus_half[:, 0:1], ALU.add)

            def power(k, n):
                done(eng, f"ag{k}", n)
                done(eng, {1: "x1d", 2: "x2d", 3: "y3d"}[k], n, 1)
                carry(3 + k)
                eng.tensor_scalar(rstd[:, k - 1, :], bn2[:, k - 1, :, 1], EPS, None, ALU.add)\
                   .then_inc(S[f"ep{k}"], 1)
                done(eng, f"ep{k}", n)
                eng.tensor_tensor(rstd[:, k - 1, :], rstd[:, k - 1, :], minus_half[:, 0:TP], ALU.pow)\
                   .then_inc(S[f"po{k}"], 1)

            eng.wait_ge(S["w_zero"], 4)
            eng.wait_ge(S["bias_in"], 32)

            def one(i, on):
                ret, gate, cross, ffn = on
                g, b, f = i - LAG_GATE, i - LAG_CROSS, i - LAG_FFN
                if isinstance(i, int) and i == 1:
                    eng.wait_ge(S["late_in"], 16 * 8)
                if cross:
                    done(eng, "x1d", b)
                    done(eng, "a2", b, 1)
                    for t in range(TP):
                        mm = eng.tensor_tensor(x1_b[:, t, :], x1[:, t, :], bfc_sb[:, :], ALU.add)
                    mm.then_inc(S["x1b"], 1)
                if ffn:
                    done(eng, "x2d", f)
                    done(eng, "a3", f, 1)
                    for t in range(TP):
                        mm = eng.tensor_tensor(x2_b[:, t, :], x2[:, t, :], b2_sb[:, :], ALU.add)
                    mm.then_inc(S["x2b"], 1)
                if gate:
                    done(eng, "veps", g)
                    done(eng, "rt", g, 1)
                    eng.tensor_tensor(y_rstd[:, :], y_var[:, :], minus_half[:, :], ALU.pow)\
                       .then_inc(S["ypow"], 1)
                if gate:
                    done(eng, "yn", g)
                    carry(8)
                    for kc in range(KC):
                        mm = eng.tensor_scalar(y_norm[:, kc, :], y_norm[:, kc, :], gn_w[:, kc:kc + 1],
                                               gn_b[:, kc:kc + 1], ALU.mult, ALU.add)
                    mm.then_inc(S["yaff"], 1)

                def gelu_low(u):
                    part = slice(2 * u, 2 * u + 2)
                    done(eng, f"hh{u}", f)
                    done(eng, "f_out", f, 1)
                    eng.tensor_tensor(h_lo[:, part, :], h_sb[:, u % 2, :, :], h_hi[:, part, :], ALU.subtract)\
                       .then_inc(S[f"hs{u}"], 1)

                if ffn:
                    gelu_low(0)
                if ret:
                    done(eng, "qk_mid", i)
                    eng.tensor_tensor(qk_part[:, 2, :, :, :], qk_swap[:, :, :, :], qk_part[:, 1, :, :, :],
                                      ALU.subtract).then_inc(S["qk_lo"], 1)
                if ffn:
                    gelu_low(1)
                    gelu_low(2)
                    gelu_low(3)
                if gate:
                    power(1, g)
                if ffn:
                    power(3, f)
                if cross:
                    power(2, b)
            iterations(eng, one)


_CONSTS = ("c_xpos", "c_decay", "c_small", "c_mats", "c_ones", "c_spread")


def kernel(x, ctx_2048, L0_attn_W_Q, L0_attn_W_K, L0_attn_W_V, L0_attn_W_G, L0_attn_W_O,
           L0_attn_gn_weight, L0_attn_gn_bias, L0_xattn_Wq, L0_xattn_Wk, L0_xattn_Wv, L0_xattn_Wfc,
           L0_xattn_bfc, L0_ffn_w1, L0_ffn_b1, L0_ffn_w2, L0_ffn_b2):
    import numpy as _np
    import concourse.bacc as _bacc
    from concourse import mybir as _mybir
    from concourse.bass_utils import run_bass_kernel_spmd as _run

    def heads(w):
        return _np.asarray(w).transpose(1, 0, 2).reshape(D, D)

    def columns(v):
        return _np.asarray(v).reshape(-1, P).T

    laid = {
        "x": _np.asarray(x).reshape(TOKENS, D), "ctx": _np.asarray(ctx_2048).reshape(TOKENS, D),
        "wq": heads(L0_attn_W_Q), "wk": heads(L0_attn_W_K), "wv": heads(L0_attn_W_V),
        "wg": _np.asarray(L0_attn_W_G), "wo": _np.asarray(L0_attn_W_O),
        "gnw": columns(L0_attn_gn_weight), "gnb": columns(L0_attn_gn_bias),
        "xwq": _np.asarray(L0_xattn_Wq).T, "xwk": _np.asarray(L0_xattn_Wk).T,
        "xwv": _np.asarray(L0_xattn_Wv).T, "xwfc": _np.asarray(L0_xattn_Wfc).T,
        "xbfc": _np.asarray(L0_xattn_bfc),
        "w1": _np.asarray(L0_ffn_w1).T, "b1": columns(L0_ffn_b1),
        "w2": _np.asarray(L0_ffn_w2).T, "b2": _np.asarray(L0_ffn_b2),
    }
    tables = shape_constants()
    laid.update({name: tables[name] for name in _CONSTS})
    nc = _bacc.Bacc("TRN2", target_bir_lowering=False, num_devices=1)
    arrays, args = {}, []
    for name, a in laid.items():
        a = _np.ascontiguousarray(a)
        arrays[f"in_{name}"] = a
        args.append(nc.dram_tensor(f"in_{name}", a.shape, _mybir.dt.from_np(a.dtype), kind="ExternalInput").ap())
    args.append(nc.dram_tensor("out_0", (TOKENS, D), F32, kind="ExternalOutput").ap())
    build(nc, *args)
    r = _run(nc, [arrays], core_ids=[0])
    return r.results[0]["out_0"].reshape(SEQS, SEQ, D)
```

```python
from contextlib import ExitStack

import numpy as np

import concourse.bass as bass
from concourse import mybir
from concourse.alu_op_type import AluOpType as ALU

F32 = mybir.dt.float32
F32R = mybir.dt.float32r
BF16 = mybir.dt.bfloat16
ACT = mybir.ActivationFunctionType
AX = mybir.AxisListType

SEQS, SEQ, D = 64, 64, 256
TOKENS = SEQS * SEQ
P = 128
KC = D // P
TB = 256
QK = 2 * KC * TB
TP = TB // P
BS = TB // SEQ
NB = TOKENS // TB
HEADS, HD = 16, 16
HC = HEADS // KC
SPLITS = ((0, 0), (0, 1), (1, 0), (0, 2), (2, 0), (1, 1))
SROWS = len(SPLITS) * HD
STACKS = sum(1 if a == b else 2 for a, b in SPLITS)
XHEADS, XG, XD = 32, 8, 8
XJ = XHEADS // XG
F = 1024
FC = F // P
EPS = 1e-5
ATTN_EPS = 1e-5
LAG_GATE, LAG_CROSS, LAG_FFN = 1, 2, 3


def shape_constants():
    f = np.float32
    half = HD // 2
    xscale = (np.arange(0, HD, 2, dtype=f) + f(0.4 * HD)) / f(1.4 * HD)
    pos = np.arange(SEQ, dtype=f)
    scale = xscale[None, :] ** (pos[:, None] / f(64))
    inv = f(1.0) / f(10000.0) ** (np.arange(half, dtype=f) / f(half))
    angle = pos[:, None] * inv[None, :]
    p = np.arange(P)
    pair = (p % HD) // 2
    sign = np.where(p % 2 == 0, f(-1), f(1))[:, None]
    xpos = np.stack([(np.cos(angle) * scale)[:, pair].T, (np.cos(angle) * (f(1) / scale))[:, pair].T,
                     sign * (np.sin(angle) * scale)[:, pair].T,
                     sign * (np.sin(angle) * (f(1) / scale))[:, pair].T], 1).astype(f)
    gammas = f(1) - np.exp(np.linspace(np.log(1.0 / 32), np.log(1.0 / 64), HEADS)).astype(f)
    b, t = p // SEQ, p % SEQ
    decay = np.zeros((P, HC, KC, P), f)
    lag = (t[None, :] - t[:, None])
    seen = (b[None, :] == b[:, None]) & (lag >= 0)
    for h in range(HC):
        for c in range(KC):
            decay[:, h, c] = np.where(seen, gammas[HC * c + h] ** np.maximum(lag, 0).astype(f), 0)
    small = np.zeros((P, XJ + HC), f)
    for j in range(XJ):
        small[:, j] = (p % 32) // XD == j
    mats = np.zeros((P, 3, P), f)
    mats[:, 0] = np.eye(P)
    for s in range(2):
        mats[:, 1 + s] = (b[:, None] == s) & (t[:, None] == t[None, :])
    ones = np.zeros((P, 2, 32), f)
    for jj in range(2):
        ones[:, jj] = np.arange(32)[None, :] // XD == 2 * jj + b[:, None]
    small[:, XJ:] = (p[:, None] // HD == np.arange(8)[None, :]) / HD
    spread = np.zeros((P, 4, P), f)
    for tc in range(4):
        for h in range(8):
            spread[8 * tc + h, tc] = p // HD == h
    return {"c_spread": spread.reshape(P, -1), "c_xpos": xpos, "c_decay": decay.reshape(P, -1), "c_small": small,
            "c_mats": mats.reshape(P, -1), "c_ones": ones.reshape(P, -1)}


def build(nc, x, ctx, wq, wk, wv, wg, wo, gnw, gnb, xwq, xwk, xwv, xwfc, xbfc, w1, b1, w2, b2,
          c_xpos, c_decay, c_small, c_mats, c_ones, c_spread, out):
    x_blocks = x.rearrange("(n t p) c -> n p t c", p=P, t=TP)
    ctx_blocks = ctx.rearrange("(n t p) c -> n p t c", p=P, t=TP)
    out_blocks = out.rearrange("(n t p) c -> n p t c", p=P, t=TP)

    scratch = nc.dram_tensor("qk_scratch", (NB, P, 3 * 2 * KC * TB), BF16, kind="Internal").ap()
    qk_blocks = scratch
    qk_heads = scratch.rearrange("n (h d) (a f) -> n d h a f", d=HD, f=KC * TB)

    stack = ExitStack()
    with stack:
        def sb(name, shape, dt=F32):
            return stack.enter_context(nc.sbuf_tensor(name, shape, dt))

        def ps(name, shape, dt=F32):
            return stack.enter_context(nc.psum_tensor(name, shape, dt))

        def sem(name):
            return stack.enter_context(nc.semaphore(name))

        NW = 6
        w_hi = sb("w_hi", [P, NW, KC, D], F32R)
        w_lo = sb("w_lo", [P, NW, KC, D], F32R)
        wxv_hi = sb("wxv_hi", [P, KC, XG * XD], F32R)
        wxv_lo = sb("wxv_lo", [P, KC, XG * XD], F32R)
        wo_sb = sb("wo_sb", [P, KC, D])
        wfc_sb = sb("wfc_sb", [P, KC, D])
        w1q = sb("w1q", [P, KC, F], F32R)
        w2q = sb("w2q", [P, FC, D], F32R)
        xpos = sb("xpos", [P, 4, SEQ])
        decay = sb("decay", [P, HC, KC, P])
        small = sb("small", [P, XJ + HC])
        spread = sb("spread", [32, 4, P])
        mats = sb("mats", [P, 3, P])
        ones = sb("ones", [P, 2, 32])
        gn_w = sb("gn_w", [P, KC])
        gn_b = sb("gn_b", [P, KC])
        b1_sb = sb("b1_sb", [P, FC])
        bfc_sb = sb("bfc_sb", [P, D])
        b2_sb = sb("b2_sb", [P, D])
        all_mean = sb("all_mean", [P, P])
        v_mean = sb("v_mean", [P, KC * HEADS])
        abs_sum = sb("abs_sum", [P, 2])
        thr = sb("thr", [P, 2, 2])

        x_in = sb("x_in", [P, TP, D])
        ctx_in = sb("ctx_in", [P, TP, D])
        x_res = sb("x_res", [P, TP, D])
        xT_hi, xT_lo = sb("xT_hi", [P, KC, TB], F32R), sb("xT_lo", [P, KC, TB], F32R)
        cT_hi, cT_lo = sb("cT_hi", [P, KC, TB], F32R), sb("cT_lo", [P, KC, TB], F32R)
        x1T_hi, x1T_lo = sb("x1T_hi", [P, KC, TB], F32R), sb("x1T_lo", [P, KC, TB], F32R)
        x2T_hi, x2T_lo = sb("x2T_hi", [P, KC, TB], F32R), sb("x2T_lo", [P, KC, TB], F32R)
        qk = sb("qk", [P, 2, KC, TB])
        qk_swap = sb("qk_swap", [P, 2, KC, TB])
        qk_part = sb("qk_part", [P, 3, 2, KC, TB], BF16)
        qk_st = sb("qk_st", [SROWS, HC, 2, KC, TB], BF16)
        v_par = sb("v_par", [P, 2, TP, D])
        rT = sb("rT", [P, HC, KC, P])
        gate_th = sb("gate_th", [P, KC, TB])
        gate_sb = sb("gate_sb", [P, KC, TB])
        y_sb = sb("y_sb", [P, KC, TB])
        y_var = sb("y_var", [P, TP * KC * 8])
        y_rstd = sb("y_rstd", [P, TP * KC * 8])
        y_rstdT = sb("y_rstdT", [TP * KC * 8, P])
        y_norm = sb("y_norm", [P, KC, TB])
        y_sq = y_norm
        carrier = sb("carrier", [P, 16])
        minus_half = sb("minus_half", [P, TP * KC * 8])
        zT = sb("zT", [P, KC, TB])
        bn6 = sb("bn6", [P, 3, TP, 6])
        bn2 = sb("bn2", [P, 3, TP, 2])
        rstd = sb("rstd", [P, 3, TP])
        x1 = sb("x1", [P, TP, D])
        x1_b = sb("x1_b", [P, TP, D])
        x2 = sb("x2", [P, TP, D])
        x2_b = sb("x2_b", [P, TP, D])
        y_out = sb("y_out", [P, TP, D])
        qx = sb("qx", [P, KC, TB])
        kx = sb("kx", [P, KC, BS, XJ, SEQ])
        vx = sb("vx", [P, TP, XG * XD])
        vx_bd = sb("vx_bd", [P, 2 * TP, XG, 2, 32])
        e_sb = sb("e_sb", [P, XHEADS, SEQ])
        e_max = sb("e_max", [P, XHEADS])
        pT = sb("pT", [P, 4, KC, 2, P])
        oT = sb("oT", [P, TP, KC, P])
        h_sb = sb("h_sb", [P, 2, 2, TB])
        h_hi, h_lo = sb("h_hi", [P, FC, TB], F32R), sb("h_lo", [P, FC, TB], F32R)
        raw = rT[:, :, :, :].rearrange("p h c s -> p (h c s)")\
            .rearrange("p (w k n) -> p w k n", w=4, k=KC)
        raw_xq = ctx_in[:, :, :]
        raw_kv = y_sb[:, :, :].rearrange("p a b -> p (a b)")[:, 0:2 * KC * XG * XD]\
            .rearrange("p (w k n) -> p w k n", w=2, k=KC)
        w1_raw = e_sb[:, :, :].rearrange("p a b -> p (a b)")
        w2_raw = pT[:, :, :, :, :].rearrange("p a b c d -> p (a b c d)")

        bank = [ps(f"bank{k}", [P, 2, 256]) for k in range(4)]
        big = ps("big", [P, 4, 2, 256])

        names = """w_in w_rest_in wf_in c_in late_in bias_in w_split w_quant1 w_quant2 w_abs w_abs_all w_thr w_zero
            w_ge w_high w_mean x_load c_load x_store qk_swapped qk_stored qk_low_stored qk_stacked
            xT cT x1T x2T q xq var k s0a s0b v g rt rx o1 f0 f1 f2 f3 t0a t0b kx_ps vx_ps s1a s1b pv0 f_out t1a t1b
            r0 pv1 vd o2 r1 av0 av
            q_ev k_ev qk_hi qk_mid qk_cos qk_sin qk_sum qk_rem qk_lo
            xTh cTh x1Th x2Th sqd qx_sb v_sb th e0a e0b e1a e1b h0 h1 h2 h3 p0a p1a vx_sb vbd y_ev
            xTl cTl x1Tl x2Tl yn rt_sb veps m0a m0b m1a m1b d0a d0b d1a d1b z gp a1 st1 ag1 x1d
            p0b p1b kx_sb rd0 rd1 o0d o1d a3 st3 ag3 y3d rm0_0 rm0_1 rm1_0 rm1_1 a2 st2 ag2 x2d
            gmove x1b x2b ypow ep1 ep2 ep3 po1 po2 po3 yaff hh0 hh1 hh2 hh3 hs0 hs1 hs2 hs3 xres""".split()
        S = {n: sem(n) for n in names}
        block = stack.enter_context(nc.Block())

        def done(eng, name, i, lag=0):
            n = i - lag
            if isinstance(n, int):
                n = min(n, NB - 1)
                if n < 0:
                    return
            eng.wait_ge(S[name], n + 1)

        def freed(eng, i, *users):
            for name, lag in users:
                n = i - lag
                if not isinstance(n, int) or 0 <= n < NB:
                    eng.wait_ge(S[name], n + 1)
                    return

        def iterations(eng, one):
            def act(i):
                return [0 <= i - lag < NB for lag in range(4)]
            for i in range(LAG_FFN + 1):
                one(i, act(i))
            with eng.Fori(0, NB - (LAG_FFN + 1)) as j:
                one(j + (LAG_FFN + 1), [True] * 4)
            for i in range(NB, NB + LAG_FFN):
                one(i, act(i))

        ident = mats[:, 0, :]

        @block.sync
        def _(eng):
            eng.dma_start(x_in[:, :, :], x_blocks[0, :, :, :]).then_inc(S["x_load"], 16)
            for k, w in enumerate((wq, wk)):
                eng.dma_start(raw[:, k, :, :], w.rearrange("(k p) n -> p k n", p=P)).then_inc(S["w_in"], 16)
            for k, w in enumerate((wv, wg)):
                eng.dma_start(raw[:, 2 + k, :, :], w.rearrange("(k p) n -> p k n", p=P))\
                   .then_inc(S["w_rest_in"], 16)
            eng.dma_start(raw_xq, xwq.rearrange("(k p) n -> p k n", p=P)).then_inc(S["w_rest_in"], 16)
            for k, w in enumerate((xwk, xwv)):
                eng.dma_start(raw_kv[:, k, :, :], w.rearrange("(k p) n -> p k n", p=P))\
                   .then_inc(S["w_rest_in"], 16)

            eng.dma_start(spread[:, :, :].rearrange("p a b -> p (a b)"), c_spread[0:32, :])\
               .then_inc(S["late_in"], 16)
            eng.dma_start(ones[:, :, :].rearrange("p a b -> p (a b)"), c_ones).then_inc(S["late_in"], 16)
            eng.dma_start(wo_sb[:, :, :], wo.rearrange("(k p) n -> p k n", p=P)).then_inc(S["late_in"], 16)
            eng.dma_start(wfc_sb[:, :, :], xwfc.rearrange("(k p) n -> p k n", p=P)).then_inc(S["late_in"], 16)
            eng.dma_start(b1_sb[:, :], b1).then_inc(S["late_in"], 16)
            eng.dma_start(decay[:, :, :, :].rearrange("p h c s -> p (h c s)"), c_decay).then_inc(S["late_in"], 16)
            eng.dma_start(gn_w[:, :], gnw).then_inc(S["late_in"], 16)
            eng.dma_start(gn_b[:, :], gnb).then_inc(S["late_in"], 16)

            def partners(src, par):
                return src[par:P:2, :, :, :]

            def one(i, on):
                ret, gate, cross, ffn = on
                if ret and not (isinstance(i, int) and i == 0):
                    done(eng, "xT", i, 1)
                    eng.dma_start(x_in[:, :, :], x_blocks[i, :, :, :]).then_inc(S["x_load"], 16)
                if isinstance(i, int) and i == 0:
                    for w_raw, w, k in ((w1_raw, w1, KC), (w2_raw, w2, FC)):
                        eng.dma_start(w_raw.rearrange("p (k n) -> p k n", k=k),
                                      w.rearrange("(k p) n -> p k n", p=P)).then_inc(S["wf_in"], 16)
                if gate:
                    n = i - LAG_GATE
                    if isinstance(n, int) and n == 0:
                        eng.wait_ge(S["w_split"], 7)
                    done(eng, "a1", n, 1)
                    eng.dma_start(x_res[:, :, :], x_blocks[n, :, :, :]).then_inc(S["xres"], 16)
                    done(eng, "cT", n, 1)
                    eng.dma_start(ctx_in[:, :, :], ctx_blocks[n, :, :, :]).then_inc(S["c_load"], 16)
                if ret:
                    done(eng, "k_ev", i)
                    done(eng, "q_ev", i)
                    done(eng, "qk_lo", i, 1)
                    for par in range(2):
                        eng.dma_start(partners(qk_swap, par), partners(qk, 1 - par))\
                           .then_inc(S["qk_swapped"], 16)
                    for step, stored, first, last in (("qk_mid", "qk_stored", 0, 2),
                                                      ("qk_lo", "qk_low_stored", 2, 3)):
                        done(eng, step, i)
                        eng.dma_start(qk_blocks[i, :, first * QK:last * QK],
                                      qk_part[:, first:last, :, :, :].rearrange("p a w k t -> p (a w k t)"))\
                           .then_inc(S[stored], 16)
                    done(eng, "r1", i, 1)
                    for low, stored in ((False, "qk_stored"), (True, "qk_low_stored")):
                        eng.wait_ge(S[stored], 16 * i + 16)
                        for n, parts in enumerate(SPLITS):
                            if (2 in parts) != low:
                                continue
                            rows = qk_st[n * HD:(n + 1) * HD, :, :, :, :].rearrange("d h w k t -> d h w (k t)")
                            if parts[0] == parts[1]:
                                first = 2 * parts[0]
                                eng.dma_start(rows, qk_heads[i, :, :, first:first + 2, :])\
                                   .then_inc(S["qk_stacked"], 16)
                                continue
                            for w in range(2):
                                eng.dma_start(rows[:, :, w, :], qk_heads[i, :, :, 2 * parts[w] + w, :])\
                                   .then_inc(S["qk_stacked"], 16)
            iterations(eng, one)

        @block.tensor
        def _(eng):
            def transposes(src, k, step):
                for c in range(KC):
                    for t in range(TP):
                        mm = eng.transpose(bank[k][:, c, t * P:(t + 1) * P],
                                           src[:, t, c * P:(c + 1) * P], ident)
                mm.then_inc(S[step], 1)

            def split_product(o, parts, last, step=None):
                for n, (w, a) in enumerate(parts):
                    mm = eng.matmul(o, w, a, start=(n == 0), stop=(n == len(parts) - 1))
                if last:
                    mm.then_inc(S[step], 1)

            def project(w, hi, lo, k, step):
                for oc in range(KC):
                    cols = slice(oc * P, (oc + 1) * P)
                    parts = [(a[:, w, kc, cols], b[:, kc, :])
                             for a, b in ((w_lo, hi), (w_hi, lo), (w_hi, hi)) for kc in range(KC)]
                    split_product(bank[k][:, oc, :], parts, oc == KC - 1, step)

            def out_rows(act, w, k, step):
                for t in range(TP):
                    for kc in range(KC):
                        mm = eng.matmul(bank[k][:, t, :], act(t, kc), w[:, kc, :],
                                        start=(kc == 0), stop=(kc == KC - 1))
                mm.then_inc(S[step], 1)

            def hidden_out(t, f, step):
                n = 0
                for fc in range(FC):
                    if t == 0 and fc % 2 == 0:
                        done(eng, f"hs{fc // 2}", f)
                    for a in (h_lo, h_hi):
                        mm = eng.matmul(bank[1][:, t, :], a[:, fc, t * P:(t + 1) * P], w2q[:, fc, :],
                                        start=(n == 0), stop=(n == 2 * FC - 1))
                        n += 1
                if step:
                    mm.then_inc(S[step], 1)

            def ret_scores(t, step):
                scores = big[:, :, :, :].rearrange("p a b c -> p (a b c)")
                for h in range(HC):
                    for c in range(KC):
                        toks = slice(t * P, (t + 1) * P)
                        mm = eng.matmul(scores[:, (h * KC + c) * P:(h * KC + c + 1) * P],
                                        qk_st[:, h, 1, c, toks], qk_st[:, h, 0, c, toks],
                                        start=True, stop=True)
                mm.then_inc(S[step], 1)

            def ret_values(t, g, step):
                for c in range(KC):
                    done(eng, f"rm{t}_{c}", g)
                    for par in range(2):
                        for r in range(4):
                            mm = eng.matmul(bank[1][32 * r:32 * r + 32, c, t * P:(t + 1) * P],
                                            v_par[:, par, t, c * P + 32 * r:c * P + 32 * r + 32],
                                            rT[:, 2 * r + par, c, :],
                                            start=(par == 0), stop=(par == 1),
                                            tile_position=(0, 32 * r))
                mm.then_inc(S[step], 1)

            def cross_scores(t, half, step):
                for r in (2 * half, 2 * half + 1):
                    for c in range(KC):
                        rows = slice(32 * r, 32 * r + 32)
                        for b in range(2):
                            tok = (2 * t + b) * SEQ
                            mm = eng.matmul(big[b * SEQ:(b + 1) * SEQ, r, c, :], qx[rows, c, tok:tok + SEQ],
                                            kx[rows, c, 2 * t + b, :, :].rearrange("p j s -> p (j s)"),
                                            start=True, stop=True)
                mm.then_inc(S[step], 1)

            def rstd_spread(g):
                done(eng, "rt_sb", g)
                for t in range(TP):
                    for c in range(KC):
                        mm = eng.matmul(bank[3][:, c, t * P:(t + 1) * P], spread[:, t * KC + c, :],
                                        y_rstdT[:, :], start=True, stop=True)
                mm.then_inc(S["rx"], 1)

            def prob_transposes(half, step):
                for r in (2 * half, 2 * half + 1):
                    for q in range(4):
                        mm = eng.transpose(big[:, r, :, :].rearrange("p a b -> p (a b)")[:, q * P:(q + 1) * P],
                                           e_sb[:, :, :].rearrange("p h s -> p (h s)")
                                           [:, (4 * r + q) * P:(4 * r + q + 1) * P], ident)
                mm.then_inc(S[step], 1)

            def prob_values(t, k, step):
                for c in range(KC):
                    for b in range(2):
                        for jj in range(2):
                            for r in range(4):
                                eng.matmul(bank[k][32 * r:32 * r + 32, 0, c * P + b * SEQ:c * P + (b + 1) * SEQ],
                                           vx_bd[:, b * TP + t, 4 * c + r, jj, :],
                                           pT[:, r, c, jj, b * SEQ:(b + 1) * SEQ],
                                           start=(jj == 0), stop=(jj == 1), tile_position=(0, 32 * r))
                    for jj in range(2):
                        for r in range(4):
                            mm = eng.matmul(bank[k][32 * r:32 * r + 32, 1, c * P:(c + 1) * P],
                                            ones[:, jj, :], pT[:, r, c, jj, :],
                                            start=(jj == 0), stop=(jj == 1), tile_position=(0, 32 * r))
                mm.then_inc(S[step], 1)

            eng.wait_ge(S["c_in"], 16 * 3)

            def one(i, on):
                ret, gate, cross, ffn = on
                g, b, f = i - LAG_GATE, i - LAG_CROSS, i - LAG_FFN

                def feed_forward(u, k):
                    for oc in range(2):
                        fc = 2 * u + oc
                        parts = [(w1q[:, kc, fc * P:(fc + 1) * P], a[:, kc, :])
                                 for a in (x2T_lo, x2T_hi) for kc in range(KC)]
                        split_product(bank[k][:, oc, :], parts, oc == 1, f"f{u}")

                if isinstance(i, int) and i == 1:
                    eng.wait_ge(S["late_in"], 16 * 8)
                    eng.wait_ge(S["w_zero"], 3)
                    eng.wait_ge(S["w_abs"], 2)
                    done(eng, "v_sb", 0)
                    eng.matmul(bank[0][:, 0, 0:2], all_mean[:, :], abs_sum[:, :], start=True, stop=True)\
                       .then_inc(S["w_abs_all"], 1)
                    eng.wait_ge(S["w_thr"], 1)
                if ret:
                    eng.wait_ge(S["x_load"], 16 * i + 16)
                    freed(eng, i, ("a1", 2), ("xTl", 1))
                    transposes(x_in, 2, "xT")
                if gate:
                    done(eng, "rm0_1", g)
                    ret_scores(1, "r1")
                    freed(eng, g, ("a3", 3), ("gp", 0))
                    ret_values(0, g, "av0")
                if cross:
                    done(eng, "vx_sb", b)
                    done(eng, "kx_sb", b)
                    for s in range(2):
                        mm = eng.matmul(bank[3][:, 1, s * P:(s + 1) * P], mats[:, 1 + s, :],
                                        vx[:, :, :].rearrange("p t c -> p (t c)"), start=True, stop=True)
                    mm.then_inc(S["vd"], 1)
                if ffn:
                    done(eng, "o1d", f)
                    out_rows(lambda t, kc: oT[:, t, kc, :], wfc_sb, 0, "o2")
                if gate:
                    ret_values(1, g, "av")
                if ret:
                    done(eng, "xTl", i)
                    if isinstance(i, int) and i == 0:
                        eng.wait_ge(S["w_split"], 2)
                    freed(eng, i, ("vbd", 2), ("q_ev", 1))
                    project(0, xT_hi, xT_lo, 3, "q")
                    freed(eng, i, ("a2", 3), ("v_sb", 1))
                    project(1, xT_hi, xT_lo, 0, "k")
                if gate:
                    eng.wait_ge(S["c_load"], 16 * g + 16)
                    done(eng, "y_ev", g)
                    transposes(ctx_in, 1, "cT")
                if cross:
                    done(eng, "x1d", b)
                    freed(eng, i, ("xTl", 0), ("a1", 2))
                    transposes(x1, 2, "x1T")
                if gate:
                    done(eng, "sqd", g)
                    freed(eng, i, ("q_ev", 0), ("vbd", 2))
                    for t in range(TP):
                        for c in range(KC):
                            mm = eng.matmul(bank[3][:, 0, (t * KC + c) * 8:(t * KC + c + 1) * 8],
                                            y_sq[:, c, t * P:(t + 1) * P], small[:, XJ:],
                                            start=True, stop=True)
                    mm.then_inc(S["var"], 1)
                if ffn:
                    done(eng, "x2d", f)
                    freed(eng, i, ("k_ev", 0), ("a2", 3))
                    transposes(x2, 0, "x2T")
                if cross:
                    done(eng, "x1Tl", b)
                    project(4, x1T_hi, x1T_lo, 2, "xq")
                if ret:
                    if isinstance(i, int) and i == 0:
                        eng.wait_ge(S["w_split"], 7)
                    freed(eng, i, ("cTl", 1), ("gp", 1))
                    project(3, xT_hi, xT_lo, 1, "g")
                if cross:
                    done(eng, "qx_sb", b)
                    done(eng, "kx_sb", b)
                    freed(eng, i, ("rm1_1", 1), ("p1a", 3))
                    cross_scores(0, 0, "s0a")
                if ret:
                    freed(eng, i, ("x2Tl", 3), ("k_ev", 0))
                    for t in range(TP):
                        parts = [(a[:, kc, t * P:(t + 1) * P], w[:, 2, kc, :])
                                 for a, w in ((xT_lo, w_hi), (xT_hi, w_lo), (xT_hi, w_hi))
                                 for kc in range(KC)]
                        split_product(bank[0][:, t, :], parts, t == TP - 1, "v")
                if gate:
                    done(eng, "ypow", g)
                    done(eng, "veps", g)
                    eng.transpose(bank[3][0:32, 0, 0:P], y_rstd[:, :], ident).then_inc(S["rt"], 1)
                if cross:
                    freed(eng, i, ("rm1_1", 1), ("p1b", 3))
                    cross_scores(0, 1, "s0b")
                if ffn:
                    if isinstance(f, int) and f == 0:
                        eng.wait_ge(S["w_quant2"], 1)
                    done(eng, "x2Tl", f)
                    freed(eng, i, ("qx_sb", 2), ("h2", 4))
                    feed_forward(0, 2)
                if cross:
                    done(eng, "e0a", b)
                    prob_transposes(0, "t0a")
                if gate:
                    rstd_spread(g)
                if ffn:
                    freed(eng, i, ("v_sb", 0), ("x2Tl", 3))
                    feed_forward(1, 0)
                if cross:
                    done(eng, "e0b", b)
                    prob_transposes(1, "t0b")
                if gate:
                    done(eng, "cTl", g)
                    done(eng, "yn", g)
                    project(5, cT_hi, cT_lo, 3, "kx_ps")
                if cross:
                    done(eng, "p0a", b)
                    cross_scores(1, 0, "s1a")
                if ffn:
                    freed(eng, i, ("h0", 3))
                    feed_forward(2, 2)
                if cross:
                    done(eng, "p0b", b)
                    cross_scores(1, 1, "s1b")
                if ffn:
                    freed(eng, i, ("gp", 0), ("cTl", 1), ("a3", 4))
                    feed_forward(3, 1)
                if gate:
                    freed(eng, i, ("h2", 3), ("qx_sb", 2), ("xTl", 0))
                    for t in range(TP):
                        parts = [(a[:, kc, t * P:(t + 1) * P], w[:, kc, :])
                                 for a, w in ((cT_lo, wxv_hi), (cT_hi, wxv_lo), (cT_hi, wxv_hi))
                                 for kc in range(KC)]
                        split_product(bank[2][:, 0, t * 64:(t + 1) * 64], parts, t == TP - 1, "vx_ps")
                if cross:
                    done(eng, "p0a", b)
                    done(eng, "p0b", b)
                    freed(eng, i, ("h1", 3), ("v_sb", 0), ("o1d", 3))
                    done(eng, "vbd", b)
                    prob_values(0, 0, "pv0")
                if ffn:
                    freed(eng, i, ("h3", 3))
                    hidden_out(0, f, None)
                    hidden_out(1, f, "f_out")
                if cross:
                    done(eng, "e1a", b)
                    prob_transposes(0, "t1a")
                    done(eng, "e1b", b)
                    prob_transposes(1, "t1b")
                if gate:
                    done(eng, "z", g)
                    done(eng, "vx_sb", g)
                    out_rows(lambda t, kc: zT[:, kc, t * P:(t + 1) * P], wo_sb, 2, "o1")
                if ret:
                    eng.wait_ge(S["qk_stacked"], 16 * STACKS * (i + 1))
                    freed(eng, i, ("p1b", 2), ("rm1_1", 1))
                    if not (isinstance(i, int) and not cross):
                        done(eng, "p1a", b)
                    ret_scores(0, "r0")
                if cross:
                    done(eng, "p1a", b)
                    done(eng, "p1b", b)
                    done(eng, "o0d", b)
                    prob_values(1, 0, "pv1")
            iterations(eng, one)

        @block.scalar
        def _(eng):
            def copy(o, a):
                return eng.activation(o, a, ACT.Copy)

            eng.dma_start(mats[:, :, :].rearrange("p a b -> p (a b)"), c_mats).then_inc(S["c_in"], 16)
            eng.dma_start(small[:, :], c_small).then_inc(S["c_in"], 16)
            eng.dma_start(xpos[:, :, :].rearrange("p a b -> p (a b)"),
                          c_xpos.rearrange("p a b -> p (a b)")).then_inc(S["c_in"], 16)

            def one(i, on):
                ret, gate, cross, ffn = on
                g, b, f = i - LAG_GATE, i - LAG_CROSS, i - LAG_FFN

                def gelu(u, k):
                    done(eng, f"f{u}", f)
                    if u < 2:
                        done(eng, f"hs{u + 2}", f, 1)
                    else:
                        done(eng, f"hs{u - 2}", f)
                    for oc in range(2):
                        fc = 2 * u + oc
                        mm = eng.activation(h_sb[:, u % 2, oc, :], bank[k][:, oc, :], ACT.Gelu,
                                            bias=b1_sb[:, fc:fc + 1])
                    mm.then_inc(S[f"h{u}"], 1)
                    done(eng, f"h{u}", f)
                    done(eng, "f_out", f, 1)
                    copy(h_hi[:, 2 * u:2 * u + 2, :], h_sb[:, u % 2, :, :]).then_inc(S[f"hh{u}"], 1)

                def exponent(t, half):
                    ab = "ab"[half]
                    done(eng, f"d{t}{ab}", b)
                    rows = e_sb[:, half * XHEADS // 2:(half + 1) * XHEADS // 2, :]
                    eng.activation(rows, rows, ACT.Exp, scale=float(XD) ** -0.5).then_inc(S[f"e{t}{ab}"], 1)

                if ret:
                    done(eng, "xT", i)
                    done(eng, "g", i, 1)
                    done(eng, "v", i, 1)
                    copy(xT_hi[:, :, :], bank[2][:, :, :]).then_inc(S["xTh"], 1)
                if cross:
                    done(eng, "vd", b)
                    done(eng, "pv1", b, 1)
                    for h in range(2):
                        rows = slice(h * SEQ, (h + 1) * SEQ)
                        src = bank[3][rows, 1, :].rearrange("p (a d) -> p a d", d=XD)
                        for jj in range(2):
                            mm = copy(vx_bd[rows, :, :, jj, (2 * jj + h) * XD:(2 * jj + h + 1) * XD]
                                      .rearrange("p a b d -> p (a b) d"), src)
                    mm.then_inc(S["vbd"], 1)
                if gate:
                    done(eng, "av", g)
                    done(eng, "var", g, 1)
                    done(eng, "yn", g, 1)
                    eng.activation(y_sq[:, :, :], bank[1][:, :, :], ACT.Square).then_inc(S["sqd"], 1)
                    copy(y_sb[:, :, :], bank[1][:, :, :]).then_inc(S["y_ev"], 1)
                if ret:
                    done(eng, "q", i)
                    done(eng, "qk_rem", i, 1)
                    copy(qk[:, 0, :, :], bank[3][:, :, :]).then_inc(S["q_ev"], 1)
                    done(eng, "k", i)
                    copy(qk[:, 1, :, :], bank[0][:, :, :]).then_inc(S["k_ev"], 1)
                if cross:
                    done(eng, "x1T", b)
                    done(eng, "xq", b, 1)
                    copy(x1T_hi[:, :, :], bank[2][:, :, :]).then_inc(S["x1Th"], 1)
                if gate:
                    done(eng, "cT", g)
                    done(eng, "vx_ps", g, 1)
                    copy(cT_hi[:, :, :], bank[1][:, :, :]).then_inc(S["cTh"], 1)
                if ffn:
                    done(eng, "x2T", f)
                    done(eng, "f3", f, 1)
                    copy(x2T_hi[:, :, :], bank[0][:, :, :]).then_inc(S["x2Th"], 1)
                if cross:
                    done(eng, "xq", b)
                    done(eng, "s1b", b, 1)
                    copy(qx[:, :, :], bank[2][:, :, :]).then_inc(S["qx_sb"], 1)
                if ret:
                    done(eng, "g", i)
                    done(eng, "gmove", i, 1)
                    eng.activation(gate_th[:, :, :], bank[1][:, :, :], ACT.Tanh, scale=0.5)\
                       .then_inc(S["th"], 1)
                if cross:
                    exponent(0, 0)
                if ret:
                    done(eng, "v", i)
                    done(eng, "av", i, 1)
                    if isinstance(i, int) and i == 0:
                        eng.wait_ge(S["w_zero"], 3)
                    for par in range(2):
                        cols = [a.rearrange("p t (h c) -> p (t h) c", c=2 * HD)[:, :, par * HD:par * HD + HD]
                                for a in (v_par[:, par, :, :], bank[0][:, :, :])]
                        mm = copy(cols[0], cols[1])
                    mm.then_inc(S["v_sb"], 1)
                    done(eng, "qk_sum", i)
                    if not (isinstance(i, int) and i == 0):
                        eng.wait_ge(S["qk_stored"], 16 * i)
                    copy(qk_part[:, 0, :, :, :], qk[:, :, :, :]).then_inc(S["qk_hi"], 1)
                if cross:
                    exponent(0, 1)
                if ret:
                    done(eng, "qk_rem", i)
                    copy(qk_part[:, 1, :, :, :], qk_swap[:, :, :, :]).then_inc(S["qk_mid"], 1)
                if cross:
                    done(eng, "t0a", b)
                    done(eng, "pv1", b, 1)
                    copy(pT[:, 0:2, :, :, :].rearrange("p r a b c -> p (r a b c)"),
                         big[:, 0:2, :, :].rearrange("p r a b -> p (r a b)")).then_inc(S["p0a"], 1)
                if ffn:
                    if isinstance(f, int) and f == 0:
                        eng.wait_ge(S["late_in"], 16 * 8)
                    gelu(0, 2)
                    gelu(1, 0)
                    gelu(2, 2)
                    gelu(3, 1)
                if gate:
                    done(eng, "vx_ps", g)
                    done(eng, "vd", g, 1)
                    copy(vx[:, :, :].rearrange("p t c -> p (t c)"), bank[2][:, 0, 0:P]).then_inc(S["vx_sb"], 1)
                    done(eng, "kx_ps", g)
                    done(eng, "s1b", g, 1)
                    for j in range(XJ):
                        mm = eng.activation(kx[:, :, :, j, :],
                                            bank[3][:, :, :].rearrange("p c (s t) -> p c s t", t=SEQ),
                                            ACT.Copy, scale=small[:, j:j + 1])
                    mm.then_inc(S["kx_sb"], 1)
                if cross:
                    exponent(1, 0)
                    exponent(1, 1)
                    done(eng, "t1a", b)
                    done(eng, "pv0", b)
                    copy(pT[:, 0:2, :, :, :].rearrange("p r a b c -> p (r a b c)"),
                         big[:, 0:2, :, :].rearrange("p r a b -> p (r a b)")).then_inc(S["p1a"], 1)
                    done(eng, "t1b", b)
                    copy(pT[:, 2:4, :, :, :].rearrange("p r a b c -> p (r a b c)"),
                         big[:, 2:4, :, :].rearrange("p r a b -> p (r a b)")).then_inc(S["p1b"], 1)
                if ret:
                    done(eng, "gp", i)
                    done(eng, "z", i, 1)
                    eng.activation(gate_sb[:, :, :], gate_th[:, :, :], ACT.Copy, scale=0.5).then_inc(S["gmove"], 1)
                if ffn:
                    done(eng, "y3d", f)
                    eng.dma_start(out_blocks[f, :, :, :], y_out[:, :, :]).then_inc(S["x_store"], 16)
            iterations(eng, one)
            eng.wait_ge(S["x_store"], 16 * NB)

        @block.vector
        def _(eng):
            def bcast(ap, axis, n):
                a = ap.unsqueeze(axis)
                shape = list(a.shape)
                shape[axis] = n
                return a.to_broadcast(shape)

            def split(k, src, step):
                eng.tensor_copy(w_hi[:, k, :, :], src).then_inc(S["w_high"], 1)
                eng.wait_ge(S["w_high"], k + 1)
                eng.tensor_tensor(w_lo[:, k, :, :], src, w_hi[:, k, :, :], ALU.subtract).then_inc(S[step], 1)

            eng.wait_ge(S["w_in"], 16 * 2)
            for k in range(2):
                split(k, raw[:, k, :, :], "w_split")

            def split_rest():
                eng.wait_ge(S["w_rest_in"], 16 * 5)
                v_heads = raw[:, 2, :, :].rearrange("p k (h d) -> p (k h) d", d=HD)
                eng.tensor_reduce(v_mean[:, :], v_heads, AX.X, ALU.add).then_inc(S["w_mean"], 1)
                eng.wait_ge(S["w_mean"], 1)
                eng.tensor_scalar(v_mean[:, :], v_mean[:, :], 1.0 / HD, None, ALU.mult).then_inc(S["w_mean"], 1)
                eng.wait_ge(S["w_mean"], 2)
                eng.tensor_tensor(v_heads, v_heads, bcast(v_mean[:, :], 2, HD), ALU.subtract)\
                   .then_inc(S["w_mean"], 1)
                eng.wait_ge(S["w_mean"], 3)
                for k, src in ((2, raw[:, 2, :, :]), (3, raw[:, 3, :, :]), (4, raw_xq)):
                    split(k, src, "w_split")
                kx_rep = bcast(raw_kv[:, 0, :, :].rearrange("p k (g d) -> p (k g) d", d=XD), 2, XJ)
                kx_hi = w_hi[:, 5, :, :].rearrange("p k (g j d) -> p (k g) j d", j=XJ, d=XD)
                kx_lo = w_lo[:, 5, :, :].rearrange("p k (g j d) -> p (k g) j d", j=XJ, d=XD)
                eng.tensor_copy(kx_hi, kx_rep).then_inc(S["w_high"], 1)
                eng.tensor_copy(wxv_hi[:, :, :], raw_kv[:, 1, :, :]).then_inc(S["w_high"], 1)
                eng.wait_ge(S["w_high"], 7)
                eng.tensor_tensor(kx_lo, kx_rep, kx_hi, ALU.subtract).then_inc(S["w_split"], 1)
                eng.tensor_tensor(wxv_lo[:, :, :], raw_kv[:, 1, :, :], wxv_hi[:, :, :], ALU.subtract)\
                   .then_inc(S["w_split"], 1)

            def weight_sums():
                eng.wait_ge(S["wf_in"], 16 * 2)
                for k, r_ in enumerate((w1_raw, w2_raw)):
                    eng.tensor_reduce(abs_sum[:, k:k + 1], r_, AX.X, ALU.add, apply_absolute_value=True)\
                       .then_inc(S["w_abs"], 1)

            def thresholds():
                eng.wait_ge(S["w_abs_all"], 1)
                eng.tensor_scalar(thr[:, 0, :], bank[0][:, 0, 0:2], 0.7, None, ALU.mult).then_inc(S["w_thr"], 1)
                eng.wait_ge(S["w_thr"], 1)
                eng.tensor_scalar(thr[:, 1, :], thr[:, 0, :], -1.0, None, ALU.mult).then_inc(S["w_thr"], 1)

            def ternary():
                eng.wait_ge(S["w_thr"], 2)
                for k, (r_, q_, s_) in enumerate((
                        (w1_raw, w1q[:, :, :].rearrange("p a b -> p (a b)"), "w_quant1"),
                        (w2_raw, w2q[:, :, :].rearrange("p a b -> p (a b)"), "w_quant2"))):
                    eng.tensor_scalar(q_, r_, thr[:, 1, k:k + 1], None, ALU.is_le).then_inc(S["w_ge"], 1)
                    eng.wait_ge(S["w_ge"], k + 1)
                    eng.scalar_tensor_tensor(out=q_, in0=r_, scalar=thr[:, 0, k:k + 1], in1=q_,
                                             op0=ALU.is_ge, op1=ALU.subtract).then_inc(S[s_], 1)

            def low_part(o, k, hi, step):
                eng.tensor_tensor(o[:, :, :], bank[k][:, :, :], hi[:, :, :], ALU.subtract).then_inc(S[step], 1)

            def times_tables(a, first, step):
                for w in range(2):
                    rows = a[:, w, :, :].rearrange("p k (s t) -> p (k s) t", t=SEQ)
                    mm = eng.tensor_tensor(rows, rows, bcast(xpos[:, first + w, :], 1, KC * BS), ALU.mult)
                mm.then_inc(S[step], 1)

            def norm_sum(k, psum_bank, residual, y):
                eng.tensor_tensor(y[:, :, :], psum_bank[:, :, :], residual[:, :, :], ALU.add)\
                   .then_inc(S[f"a{k}"], 1)

            def norm_stats(k, y, n):
                done(eng, f"a{k}", n)
                for t in range(TP):
                    mm = eng.bn_stats(bn6[:, k - 1, t, :], y[:, t, :])
                mm.then_inc(S[f"st{k}"], 1)
                done(eng, f"st{k}", n)
                eng.memset(carrier[:, k:k + 1], 0.0)
                for t in range(TP):
                    mm = eng.bn_aggr(bn2[:, k - 1, t, :], bn6[:, k - 1, t, :])
                mm.then_inc(S[f"ag{k}"], 1)

            def norm_apply(k, y, n, y_done):
                done(eng, f"po{k}", n)
                for t in range(TP):
                    mm = eng.tensor_scalar(y[:, t, :], y[:, t, :], bn2[:, k - 1, t, 0:1],
                                           rstd[:, k - 1, t:t + 1], ALU.subtract, ALU.mult)
                mm.then_inc(S[y_done], 1)

            def softmax_shift(t, b, half):
                ab = "ab"[half]
                heads = slice(half * XHEADS // 2, (half + 1) * XHEADS // 2)
                done(eng, f"s{t}{ab}", b)
                rows = big[:, 2 * half:2 * half + 2, :, :].rearrange("p r c (j s) -> p (r c j) s", s=SEQ)
                eng.tensor_reduce(e_max[:, heads], rows, AX.X, ALU.max).then_inc(S[f"m{t}{ab}"], 1)
                done(eng, f"m{t}{ab}", b)
                if t == 0:
                    done(eng, f"t1{ab}", b, 1)
                else:
                    done(eng, f"t0{ab}", b)
                eng.tensor_tensor(e_sb[:, heads, :], rows, bcast(e_max[:, heads], 2, SEQ), ALU.subtract)\
                   .then_inc(S[f"d{t}{ab}"], 1)

            def probs_out(b):
                done(eng, "t0b", b)
                done(eng, "pv1", b, 1)
                eng.tensor_copy(pT[:, 2:4, :, :, :].rearrange("p r a b c -> p (r a b c)"),
                                big[:, 2:4, :, :].rearrange("p r a b -> p (r a b)")).then_inc(S["p0b"], 1)

            def normalize(t, b):
                done(eng, f"pv{t}", b)
                den = bank[0][:, 1, :].rearrange("p (c s) -> p c s", c=KC)
                num = bank[0][:, 0, :].rearrange("p (c s) -> p c s", c=KC)
                done(eng, "o2", b, 1)
                eng.reciprocal(oT[:, t, :, :], den).then_inc(S[f"rd{t}"], 1)
                done(eng, f"rd{t}", b)
                eng.tensor_tensor(oT[:, t, :, :], num, oT[:, t, :, :], ALU.mult).then_inc(S[f"o{t}d"], 1)

            def decayed(t, i):
                done(eng, f"r{t}", i)
                if t == 0:
                    done(eng, "av", i, 1)
                else:
                    done(eng, "av0", i)
                scores = big[:, :, :, :].rearrange("p r x (c s) -> p (r x) c s", c=KC)
                for c in range(KC):
                    eng.tensor_tensor(rT[:, :, c, :], scores[:, :, c, :], decay[:, :, c, :], ALU.mult)\
                       .then_inc(S[f"rm{t}_{c}"], 1)

            def one(i, on):
                ret, gate, cross, ffn = on
                g, b, f = i - LAG_GATE, i - LAG_CROSS, i - LAG_FFN
                if isinstance(i, int) and i == 1:
                    thresholds()
                if ffn:
                    normalize(1, f)
                if gate:
                    decayed(1, g)
                if ret:
                    done(eng, "xTh", i)
                    done(eng, "g", i, 1)
                    done(eng, "v", i, 1)
                    low_part(xT_lo, 2, xT_hi, "xTl")
                if isinstance(i, int) and i == 0:
                    split_rest()
                if isinstance(i, int) and i == 1:
                    ternary()
                if cross:
                    norm_stats(1, x1, b)
                if ffn:
                    done(eng, "o2", f)
                    done(eng, "x1b", f)
                    done(eng, "x2T", f, 1)
                    done(eng, "x2b", f, 1)
                    norm_sum(2, bank[0], x1_b, x2)
                    norm_stats(2, x2, f)
                if cross:
                    norm_apply(1, x1, b, "x1d")
                if ffn:
                    norm_apply(2, x2, f, "x2d")
                if cross:
                    done(eng, "x1Th", b)
                    done(eng, "xq", b, 1)
                    low_part(x1T_lo, 2, x1T_hi, "x1Tl")
                if gate:
                    done(eng, "var", g)
                    done(eng, "ypow", g, 1)
                    eng.tensor_scalar(y_var[:, :], bank[3][:, 0, 0:TP * KC * 8], ATTN_EPS, None, ALU.add)\
                       .then_inc(S["veps"], 1)
                    done(eng, "cTh", g)
                    done(eng, "vx_ps", g, 1)
                    low_part(cT_lo, 1, cT_hi, "cTl")
                if ffn:
                    done(eng, "x2Th", f)
                    done(eng, "f3", f, 1)
                    low_part(x2T_lo, 0, x2T_hi, "x2Tl")
                if ret:
                    if isinstance(i, int) and i == 0:
                        eng.wait_ge(S["c_in"], 16 * 3)
                    eng.wait_ge(S["qk_swapped"], 32 * i + 32)
                    times_tables(qk, 0, "qk_cos")
                    times_tables(qk_swap, 2, "qk_sin")
                if cross:
                    softmax_shift(0, b, 0)
                if ret:
                    done(eng, "qk_cos", i)
                    done(eng, "qk_sin", i)
                    eng.tensor_tensor(qk[:, :, :, :], qk[:, :, :, :], qk_swap[:, :, :, :], ALU.add)\
                       .then_inc(S["qk_sum"], 1)
                if gate:
                    done(eng, "rt", g)
                    done(eng, "rx", g, 1)
                    eng.tensor_copy(y_rstdT[:, :], bank[3][0:32, 0, 0:P]).then_inc(S["rt_sb"], 1)
                if cross:
                    softmax_shift(0, b, 1)
                if ret:
                    done(eng, "qk_hi", i)
                    eng.tensor_tensor(qk_swap[:, :, :, :], qk[:, :, :, :], qk_part[:, 0, :, :, :],
                                      ALU.subtract).then_inc(S["qk_rem"], 1)
                if gate:
                    done(eng, "rx", g)
                    done(eng, "z", g, 1)
                    eng.tensor_tensor(y_norm[:, :, :], y_sb[:, :, :], bank[3][:, :, :], ALU.mult)\
                       .then_inc(S["yn"], 1)
                if ret:
                    done(eng, "th", i)
                    eng.scalar_tensor_tensor(out=gate_th[:, :, :], in0=gate_th[:, :, :], scalar=1.0,
                                             in1=bank[1][:, :, :], op0=ALU.add, op1=ALU.mult)\
                       .then_inc(S["gp"], 1)
                if cross:
                    probs_out(b)
                    softmax_shift(1, b, 0)
                    softmax_shift(1, b, 1)
                    normalize(0, b)
                if ffn:
                    done(eng, "f_out", f)
                    done(eng, "x2b", f)
                    if not (isinstance(f, int) and f == 0):
                        eng.wait_ge(S["x_store"], 16 * f)
                    norm_sum(3, bank[1], x2_b, y_out)
                    norm_stats(3, y_out, f)
                    norm_apply(3, y_out, f, "y3d")
                if gate:
                    done(eng, "o1", g)
                    eng.wait_ge(S["xres"], 16 * g + 16)
                    done(eng, "x1T", g, 1)
                    done(eng, "x1b", g, 1)
                    norm_sum(1, bank[2], x_res, x1)
                if isinstance(i, int) and i == 0:
                    weight_sums()
                if ret:
                    if isinstance(i, int) and i == 0:
                        eng.wait_ge(S["late_in"], 16 * 8)
                    decayed(0, i)
            iterations(eng, one)

        @block.gpsimd
        def _(eng):
            eng.memset(all_mean[:, :], 1.0 / (F * D)).then_inc(S["w_zero"], 1)
            eng.memset(v_par[:, :, :, :].rearrange("p a b c -> p (a b c)"), 0.0).then_inc(S["w_zero"], 1)
            eng.memset(vx_bd[:, :, :, :, :].rearrange("p a b c d -> p (a b c d)"), 0.0)\
               .then_inc(S["w_zero"], 1)
            eng.dma_start(bfc_sb[:, :], xbfc.partition_broadcast(P)).then_inc(S["bias_in"], 16)
            eng.dma_start(b2_sb[:, :], b2.partition_broadcast(P)).then_inc(S["bias_in"], 16)
            eng.memset(minus_half[:, :], -0.5).then_inc(S["w_zero"], 1)

            def carry(place):
                eng.tensor_tensor(carrier[:, place:place + 1], minus_half[:, 0:1], minus_half[:, 0:1], ALU.add)

            def power(k, n):
                done(eng, f"ag{k}", n)
                done(eng, {1: "x1d", 2: "x2d", 3: "y3d"}[k], n, 1)
                carry(3 + k)
                eng.tensor_scalar(rstd[:, k - 1, :], bn2[:, k - 1, :, 1], EPS, None, ALU.add)\
                   .then_inc(S[f"ep{k}"], 1)
                done(eng, f"ep{k}", n)
                eng.tensor_tensor(rstd[:, k - 1, :], rstd[:, k - 1, :], minus_half[:, 0:TP], ALU.pow)\
                   .then_inc(S[f"po{k}"], 1)

            eng.wait_ge(S["w_zero"], 4)
            eng.wait_ge(S["bias_in"], 32)

            def one(i, on):
                ret, gate, cross, ffn = on
                g, b, f = i - LAG_GATE, i - LAG_CROSS, i - LAG_FFN
                if isinstance(i, int) and i == 1:
                    eng.wait_ge(S["late_in"], 16 * 8)
                if cross:
                    power(1, b)
                if ffn:
                    power(2, f)
                if gate:
                    done(eng, "veps", g)
                    done(eng, "rt", g, 1)
                    eng.tensor_tensor(y_rstd[:, :], y_var[:, :], minus_half[:, :], ALU.pow)\
                       .then_inc(S["ypow"], 1)
                if cross:
                    done(eng, "x1d", b)
                    done(eng, "a2", b, 1)
                    for t in range(TP):
                        mm = eng.tensor_tensor(x1_b[:, t, :], x1[:, t, :], bfc_sb[:, :], ALU.add)
                    mm.then_inc(S["x1b"], 1)
                if ffn:
                    done(eng, "x2d", f)
                    done(eng, "a3", f, 1)
                    for t in range(TP):
                        mm = eng.tensor_tensor(x2_b[:, t, :], x2[:, t, :], b2_sb[:, :], ALU.add)
                    mm.then_inc(S["x2b"], 1)
                if gate:
                    done(eng, "yn", g)
                    carry(8)
                    for kc in range(KC):
                        mm = eng.tensor_scalar(y_norm[:, kc, :], y_norm[:, kc, :], gn_w[:, kc:kc + 1],
                                               gn_b[:, kc:kc + 1], ALU.mult, ALU.add)
                    mm.then_inc(S["yaff"], 1)

                    done(eng, "yaff", g)
                    done(eng, "gmove", g)
                    done(eng, "o1", g, 1)
                    eng.tensor_tensor(zT[:, :, :], gate_sb[:, :, :], y_norm[:, :, :], ALU.mult)\
                       .then_inc(S["z"], 1)
                def gelu_low(u):
                    part = slice(2 * u, 2 * u + 2)
                    done(eng, f"hh{u}", f)
                    done(eng, "f_out", f, 1)
                    eng.tensor_tensor(h_lo[:, part, :], h_sb[:, u % 2, :, :], h_hi[:, part, :], ALU.subtract)\
                       .then_inc(S[f"hs{u}"], 1)

                if ret:
                    done(eng, "qk_mid", i)
                    if not (isinstance(i, int) and i == 0):
                        eng.wait_ge(S["qk_low_stored"], 16 * i)
                    eng.tensor_tensor(qk_part[:, 2, :, :, :], qk_swap[:, :, :, :], qk_part[:, 1, :, :, :],
                                      ALU.subtract).then_inc(S["qk_lo"], 1)
                if ffn:
                    gelu_low(0)
                    gelu_low(1)
                    gelu_low(2)
                    gelu_low(3)
                    power(3, f)
            iterations(eng, one)


_CONSTS = ("c_xpos", "c_decay", "c_small", "c_mats", "c_ones", "c_spread")


def kernel(x, ctx_2048, L0_attn_W_Q, L0_attn_W_K, L0_attn_W_V, L0_attn_W_G, L0_attn_W_O,
           L0_attn_gn_weight, L0_attn_gn_bias, L0_xattn_Wq, L0_xattn_Wk, L0_xattn_Wv, L0_xattn_Wfc,
           L0_xattn_bfc, L0_ffn_w1, L0_ffn_b1, L0_ffn_w2, L0_ffn_b2):
    import numpy as _np
    import concourse.bacc as _bacc
    from concourse import mybir as _mybir
    from concourse.bass_utils import run_bass_kernel_spmd as _run

    def heads(w):
        return _np.asarray(w).transpose(1, 0, 2).reshape(D, D)

    def columns(v):
        return _np.asarray(v).reshape(-1, P).T

    laid = {
        "x": _np.asarray(x).reshape(TOKENS, D), "ctx": _np.asarray(ctx_2048).reshape(TOKENS, D),
        "wq": heads(L0_attn_W_Q), "wk": heads(L0_attn_W_K), "wv": heads(L0_attn_W_V),
        "wg": _np.asarray(L0_attn_W_G), "wo": _np.asarray(L0_attn_W_O),
        "gnw": columns(L0_attn_gn_weight), "gnb": columns(L0_attn_gn_bias),
        "xwq": _np.asarray(L0_xattn_Wq).T, "xwk": _np.asarray(L0_xattn_Wk).T,
        "xwv": _np.asarray(L0_xattn_Wv).T, "xwfc": _np.asarray(L0_xattn_Wfc).T,
        "xbfc": _np.asarray(L0_xattn_bfc),
        "w1": _np.asarray(L0_ffn_w1).T, "b1": columns(L0_ffn_b1),
        "w2": _np.asarray(L0_ffn_w2).T, "b2": _np.asarray(L0_ffn_b2),
    }
    tables = shape_constants()
    laid.update({name: tables[name] for name in _CONSTS})
    nc = _bacc.Bacc("TRN2", target_bir_lowering=False, num_devices=1)
    arrays, args = {}, []
    for name, a in laid.items():
        a = _np.ascontiguousarray(a)
        arrays[f"in_{name}"] = a
        args.append(nc.dram_tensor(f"in_{name}", a.shape, _mybir.dt.from_np(a.dtype), kind="ExternalInput").ap())
    args.append(nc.dram_tensor("out_0", (TOKENS, D), F32, kind="ExternalOutput").ap())
    build(nc, *args)
    r = _run(nc, [arrays], core_ids=[0])
    return r.results[0]["out_0"].reshape(SEQS, SEQ, D)
```
